# Optimizing a Trainium2 kernel written in Bass

```python
import numpy as np
import jax
import jax.numpy as jnp

def _softmax(x, axis=-1):
    return jax.nn.softmax(x, axis=axis)

def _gelu(x):
    return jax.nn.gelu(x, approximate=True)

def _silu(x):
    return jax.nn.silu(x)

def _sigmoid(x):
    return jax.nn.sigmoid(x)

def _layernorm(x, axis=-1, eps=1e-05):
    m = jnp.mean(x, axis=axis, keepdims=True)
    v = jnp.var(x, axis=axis, keepdims=True)
    return (x - m) / jnp.sqrt(v + eps)

def _scatter_add(tgt, idx, src, axis=0):
    return tgt.at[idx].add(src)

def _segment_sum(src, seg, n):
    return jax.ops.segment_sum(src, seg, n)
kernel_name = 'mk_flamingo_gated_d4_seqx_r4_6e77a0'

def setup_inputs(seed: int=0):
    np.random.seed(seed)
    _w = jnp.asarray

    def _rec_inputs():
        import jax
        import jax.numpy as jnp
        _rk = jax.random.key(seed)
        x = 7.22e-05 + 1 * jax.random.normal(jax.random.fold_in(_rk, 1), (4, 512, 512), jnp.float32)
        _lenS = 512 - jax.random.randint(jax.random.fold_in(_rk, 7), (4,), 0, max(1, 512 // 4) + 1, jnp.int32)
        _lenS2 = 512 - jax.random.randint(jax.random.fold_in(_rk, 8), (4,), 0, max(1, 512 // 4) + 1, jnp.int32)
        _ctx_1024P = jax.random.normal(jax.random.fold_in(_rk, 11), (4, 16, 256), jnp.float32)
        _ctx_1024c = jax.random.dirichlet(jax.random.fold_in(_rk, 511), 0.3 * jnp.ones((16,), jnp.float32), (4, 512))
        _ctx_1024t = jnp.einsum('bsk,bkd->bsd', _ctx_1024c, _ctx_1024P)
        _ctx_1024t = _ctx_1024t * jax.lax.rsqrt(jnp.mean(jnp.square(_ctx_1024t)) + 1e-12) * 0.953939
        ctx_1024 = 2.81802e-05 + 1.00001 * (_ctx_1024t + 0.3 * jax.random.normal(jax.random.fold_in(_rk, 611), (4, 512, 256), jnp.float32))
        fside_BxSx2_0 = jax.random.uniform(jax.random.fold_in(_rk, 12), (4, 512, 2), jnp.float32, 0.0, 0.999707)
        _g = jax.random.normal(jax.random.fold_in(_rk, 9001), (2, 4), jnp.float32)
        _g = jnp.sign(_g) * jnp.maximum(jnp.abs(_g), 1.0) + (_g == 0) * 1.0
        g_xattn = _g[0]
        g_ffn = _g[1]
        return (x, ctx_1024, fside_BxSx2_0, g_xattn, g_ffn)
    x, ctx_1024, fside_BxSx2_0, g_xattn, g_ffn = _rec_inputs()

    def _L0_xattn_setup():
        import jax, jax.numpy as jnp
        import numpy as np
        key = jax.random.key(seed)
        ks = jax.random.split(key, 6)
        B, L, N, C, D = (8, 128, 512, 256, 128)
        return {'teacher_logits': jax.random.normal(ks[0], (B, L, N), dtype=jnp.float32), 'teacher_features': jax.random.normal(ks[1], (B, N, C), dtype=jnp.float32), 'Wq': jax.random.normal(ks[2], (D, C), dtype=jnp.float32) * (1.0 / np.sqrt(C)), 'bq': jnp.zeros((D,), dtype=jnp.float32), 'Wk': jax.random.normal(ks[3], (D, C), dtype=jnp.float32) * (1.0 / np.sqrt(C)), 'bk': jnp.zeros((D,), dtype=jnp.float32)}
    _L0_xattn_all = _L0_xattn_setup()
    _L0_xattn_in = {k: v for k, v in _L0_xattn_all.items() if k in ('Wq', 'bq', 'Wk', 'bk')}
    del _L0_xattn_all

    def _L0_ffn_setup():
        import jax, jax.numpy as jnp
        import numpy as np
        DIM = 512
        N_EXPERTS = 8
        TOP_K = 2
        key = jax.random.key(seed)
        ks = jax.random.split(key, 5)
        x = jax.random.normal(ks[0], (4, 1024, DIM), dtype=jnp.float32)
        W_up = jax.random.normal(ks[1], (DIM, DIM), dtype=jnp.float32) * (1.0 / np.sqrt(DIM))
        W_down = jax.random.normal(ks[2], (DIM, DIM), dtype=jnp.float32) * (1.0 / np.sqrt(DIM))
        W_gate = jax.random.normal(ks[3], (N_EXPERTS, DIM), dtype=jnp.float32) * (1.0 / np.sqrt(DIM))
        W_expert = jax.random.normal(ks[4], (DIM, DIM), dtype=jnp.float32) * (1.0 / np.sqrt(DIM))
        return {'x': x, 'W_up': W_up, 'W_down': W_down, 'W_gate': W_gate, 'W_expert': W_expert}
    _L0_ffn_all = _L0_ffn_setup()
    _L0_ffn_in = {k: v for k, v in _L0_ffn_all.items() if k in ('W_up', 'W_down', 'W_gate', 'W_expert')}
    del _L0_ffn_all

    def _L1_xattn_setup():
        import jax, jax.numpy as jnp
        import numpy as np
        DIM = 512
        CTX_DIM = 256
        N_HEADS = 32
        HEAD_DIM = DIM // N_HEADS
        POS_DIM = 2
        B, N, CTXN = (2, 512, 512)
        ROPE_BASE = 10000.0

        def apply_axial_rope(x, pos):
            b, n, h, d = x.shape
            p = pos.shape[-1]
            dpa = d // p
            half = dpa // 2
            freqs = ROPE_BASE ** (-jnp.arange(half, dtype=x.dtype) / half)
            ang = pos[..., :, None] * freqs
            cos = jnp.cos(ang)[:, :, None, :, :]
            sin = jnp.sin(ang)[:, :, None, :, :]
            xr = x.reshape(b, n, h, p, half, 2)
            x1, x2 = (xr[..., 0], xr[..., 1])
            out = jnp.stack([x1 * cos - x2 * sin, x1 * sin + x2 * cos], axis=-1)
            return out.reshape(b, n, h, d)
        key = jax.random.key(seed)
        ks = jax.random.split(key, 8)
        x = jax.random.normal(ks[0], (B, N, DIM), jnp.float32)
        ctx = jax.random.normal(ks[1], (B, CTXN, CTX_DIM), jnp.float32)
        pos_map = jax.random.uniform(ks[2], (B, N, POS_DIM), jnp.float32)
        ctx_pos_map = jax.random.uniform(ks[3], (B, CTXN, POS_DIM), jnp.float32)
        Wq = jax.random.normal(ks[4], (DIM, DIM), jnp.float32) / np.sqrt(DIM)
        Wkv = jax.random.normal(ks[5], (CTX_DIM, 2 * DIM), jnp.float32) / np.sqrt(CTX_DIM)
        Wout = jax.random.normal(ks[6], (DIM, DIM), jnp.float32) / np.sqrt(DIM)
        bout = jnp.zeros((DIM,), jnp.float32)
        return {'x': x, 'ctx': ctx, 'pos_map': pos_map, 'ctx_pos_map': ctx_pos_map, 'Wq': Wq, 'Wkv': Wkv, 'Wout': Wout, 'bout': bout}
    _L1_xattn_all = _L1_xattn_setup()
    _L1_xattn_in = {k: v for k, v in _L1_xattn_all.items() if k in ('Wq', 'Wkv', 'Wout', 'bout')}
    del _L1_xattn_all

    def _L1_ffn_setup():
        import jax, jax.numpy as jnp
        import numpy as np
        ACT_BITS = 8
        EPS = 1e-05

        def act_quant(x, bits=ACT_BITS):
            qb = float(2 ** (bits - 1))
            scale = qb / jnp.clip(jnp.max(jnp.abs(x), axis=-1, keepdims=True), EPS)
            xq = jnp.clip(jnp.round(x * scale), -qb, qb - 1) / scale
            return x + jax.lax.stop_gradient(xq - x)

        def weight_quant(w):
            scale = 1.0 / jnp.clip(jnp.mean(jnp.abs(w)), EPS)
            wq = jnp.clip(jnp.round(w * scale), -1.0, 1.0) / scale
            return w + jax.lax.stop_gradient(wq - w)

        def fwht(x):
            shape = x.shape
            n = shape[-1]
            x = x.reshape(-1, n)
            h = 1
            while h < n:
                x = x.reshape(-1, n // (2 * h), 2, h)
                a, b = (x[..., 0, :], x[..., 1, :])
                x = jnp.stack([a + b, a - b], axis=-2).reshape(-1, n)
                h *= 2
            return (x * (1.0 / np.sqrt(n)).astype(np.float32)).reshape(shape)

        def bitlinear(x, w):
            return jnp.einsum('bsh,oh->bso', act_quant(x), weight_quant(w))

        def h_bitlinear(x, w):
            return jnp.einsum('bsh,oh->bso', act_quant(fwht(x)), weight_quant(w))
        key = jax.random.key(seed)
        k1, k2, k3, k4 = jax.random.split(key, 4)
        H, I = (512, 2048)
        B, S = (4, 512)
        std_in = 1.0 / np.sqrt(H)
        std_mid = 1.0 / np.sqrt(I)
        return {'x': jax.random.normal(k1, (B, S, H), dtype=jnp.float32), 'w_gate': jax.random.normal(k2, (I, H), dtype=jnp.float32) * std_in, 'w_up': jax.random.normal(k3, (I, H), dtype=jnp.float32) * std_in, 'w_down': jax.random.normal(k4, (H, I), dtype=jnp.float32) * std_mid}
    _L1_ffn_all = _L1_ffn_setup()
    _L1_ffn_in = {k: v for k, v in _L1_ffn_all.items() if k in ('w_gate', 'w_up', 'w_down')}
    del _L1_ffn_all

    def _L2_xattn_setup():
        import jax, jax.numpy as jnp
        import numpy as np
        EPS = 1e-05

        def rmsnorm(x, g, eps=EPS):
            var = jnp.mean(jnp.square(x), axis=-1, keepdims=True)
            return x * jax.lax.rsqrt(var + eps) * g
        key = jax.random.key(seed)
        ks = jax.random.split(key, 8)
        B, Sq, Skv = (2, 1024, 128)
        dim, cdim, H, D = (512, 256, 16, 128)
        inner = H * D
        s = lambda f: 1.0 / np.sqrt(f)
        return {'hidden_states': jax.random.normal(ks[0], (B, Sq, dim), jnp.float32), 'encoder_hidden_states': jax.random.normal(ks[1], (B, Skv, cdim), jnp.float32), 'Wq': jax.random.normal(ks[2], (dim, inner), jnp.float32) * s(dim), 'Wk': jax.random.normal(ks[3], (cdim, inner), jnp.float32) * s(cdim), 'Wv': jax.random.normal(ks[4], (cdim, inner), jnp.float32) * s(cdim), 'Wo': jax.random.normal(ks[5], (inner, dim), jnp.float32) * s(inner), 'gq': jnp.ones((D,), jnp.float32), 'gk': jnp.ones((D,), jnp.float32)}
    _L2_xattn_all = _L2_xattn_setup()
    _L2_xattn_in = {k: v for k, v in _L2_xattn_all.items() if k in ('Wq', 'Wk', 'Wv', 'Wo', 'gq', 'gk')}
    del _L2_xattn_all

    def _L2_ffn_setup():
        import jax, jax.numpy as jnp
        import numpy as np
        H = 512
        I = 256
        E = 8
        TOP_K = 2
        IS = 1024
        B, S = (2, 512)

        def _moe_forward(hidden_states, w_router, wg, wu, wd, sw_gate, sw_up, sw_down, gate_w):
            b, s, h = hidden_states.shape
            x = hidden_states.reshape(-1, h)
            t = x.shape[0]
            shared = jax.nn.silu(x @ sw_gate.T) * (x @ sw_up.T) @ sw_down.T
            logits = x @ w_router.T
            probs = jax.nn.softmax(logits.astype(jnp.float32), axis=-1)
            top_v, top_i = jax.lax.top_k(probs, TOP_K)
            top_v = top_v / jnp.sum(top_v, axis=-1, keepdims=True)
            top_v = top_v.astype(probs.dtype)
            combine = jnp.zeros((t, probs.shape[-1]), x.dtype).at[jnp.arange(t)[:, None], top_i].add(top_v)
            g = jax.nn.silu(jnp.einsum('th,eih->tei', x, wg))
            u = jnp.einsum('th,eih->tei', x, wu)
            y = jnp.einsum('tei,ehi->teh', g * u, wd)
            expert_out = jnp.einsum('teh,te->th', y, combine)
            shared = jax.nn.sigmoid(x @ gate_w.T) * shared
            out = expert_out + shared
            return out.reshape(b, s, h)
        key = jax.random.key(seed)
        ks = jax.random.split(key, 10)
        sc_h = 1.0 / np.sqrt(H)
        sc_i = 1.0 / np.sqrt(I)
        sc_is = 1.0 / np.sqrt(IS)
        return {'hidden_states': jax.random.normal(ks[0], (B, S, H), jnp.float32), 'w_router': jax.random.normal(ks[1], (E, H), jnp.float32) * sc_h, 'wg': jax.random.normal(ks[2], (E, I, H), jnp.float32) * sc_h, 'wu': jax.random.normal(ks[3], (E, I, H), jnp.float32) * sc_h, 'wd': jax.random.normal(ks[4], (E, H, I), jnp.float32) * sc_i, 'sw_gate': jax.random.normal(ks[5], (IS, H), jnp.float32) * sc_h, 'sw_up': jax.random.normal(ks[6], (IS, H), jnp.float32) * sc_h, 'sw_down': jax.random.normal(ks[7], (H, IS), jnp.float32) * sc_is, 'gate_w': jax.random.normal(ks[8], (1, H), jnp.float32) * sc_h}
    _L2_ffn_all = _L2_ffn_setup()
    _L2_ffn_in = {k: v for k, v in _L2_ffn_all.items() if k in ('w_router', 'wg', 'wu', 'wd', 'sw_gate', 'sw_up', 'sw_down', 'gate_w')}
    del _L2_ffn_all

    def _L3_xattn_setup():
        import jax, jax.numpy as jnp
        import numpy as np
        B_, L_, D_MODEL = (4, 512, 256)
        D_STATE, D_CONV, EXPAND = (16, 4, 2)
        D_INNER = EXPAND * D_MODEL
        DT_RANK = (D_MODEL + 15) // 16

        def silu(x):
            return x * jax.nn.sigmoid(x)
        key = jax.random.key(seed)
        ks = jax.random.split(key, 10)
        f32 = jnp.float32
        hidden_states = jax.random.normal(ks[0], (B_, L_, D_MODEL), dtype=f32)
        z = jax.random.normal(ks[1], (B_, D_INNER, L_), dtype=f32)
        in_proj_w = jax.random.normal(ks[2], (D_INNER, D_MODEL), dtype=f32) * 0.02
        conv_w = jax.random.normal(ks[3], (D_INNER, 1, D_CONV), dtype=f32) * 0.1
        conv_b = jax.random.normal(ks[4], (D_INNER,), dtype=f32) * 0.02
        x_proj_w = jax.random.normal(ks[5], (DT_RANK + 2 * D_STATE, D_INNER), dtype=f32) * 0.02
        dt_proj_w = jax.random.uniform(ks[6], (D_INNER, DT_RANK), dtype=f32, minval=-DT_RANK ** (-0.5), maxval=DT_RANK ** (-0.5))
        dt = jnp.exp(jax.random.uniform(ks[7], (D_INNER,), dtype=f32, minval=np.log(0.001), maxval=np.log(0.1)))
        dt_proj_b = jnp.log(jnp.expm1(dt))
        A_log = jnp.log(jnp.broadcast_to(jnp.arange(1, D_STATE + 1, dtype=f32), (D_INNER, D_STATE)))
        D = jnp.ones((D_INNER,), f32)
        return {'hidden_states': hidden_states, 'z': z, 'in_proj_w': in_proj_w, 'conv_w': conv_w, 'conv_b': conv_b, 'x_proj_w': x_proj_w, 'dt_proj_w': dt_proj_w, 'dt_proj_b': dt_proj_b, 'A_log': A_log, 'D': D}
    _L3_xattn_all = _L3_xattn_setup()
    _L3_xattn_in = {k: v for k, v in _L3_xattn_all.items() if k in ('in_proj_w', 'conv_w', 'conv_b', 'x_proj_w', 'dt_proj_w', 'dt_proj_b', 'A_log', 'D')}
    del _L3_xattn_all

    def _L3_ffn_setup():
        import jax, jax.numpy as jnp
        import numpy as np
        BLOCK = 128
        MAXVAL = 448.0

        def _quant_dequant(x_flat):
            xb = x_flat.reshape(-1, BLOCK)
            s = jnp.max(jnp.abs(xb), axis=1, keepdims=True) / MAXVAL
            q = (xb / s).astype(jnp.float8_e4m3fn)
            return (q.astype(jnp.float32) * s).reshape(x_flat.shape)
        key = jax.random.key(seed)
        k1, k2 = jax.random.split(key)
        B, T, D, OUT = (4, 1024, 512, 512)
        x = jax.random.normal(k1, (B, T, D), dtype=jnp.float32)
        limit = float(np.sqrt(6.0 / (D + OUT)))
        weight = jax.random.uniform(k2, (OUT, D), minval=-limit, maxval=limit, dtype=jnp.float32)
        return {'x': x, 'weight': weight}
    _L3_ffn_all = _L3_ffn_setup()
    _L3_ffn_in = {k: v for k, v in _L3_ffn_all.items() if k in ('weight',)}
    del _L3_ffn_all
    return {'x': x, 'ctx_1024': ctx_1024, 'fside_BxSx2_0': fside_BxSx2_0, 'g_xattn': g_xattn, 'g_ffn': g_ffn, 'L0_xattn_Wq': _L0_xattn_in['Wq'], 'L0_xattn_bq': _L0_xattn_in['bq'], 'L0_xattn_Wk': _L0_xattn_in['Wk'], 'L0_xattn_bk': _L0_xattn_in['bk'], 'L0_ffn_W_up': _L0_ffn_in['W_up'], 'L0_ffn_W_down': _L0_ffn_in['W_down'], 'L0_ffn_W_gate': _L0_ffn_in['W_gate'], 'L0_ffn_W_expert': _L0_ffn_in['W_expert'], 'L1_xattn_Wq': _L1_xattn_in['Wq'], 'L1_xattn_Wkv': _L1_xattn_in['Wkv'], 'L1_xattn_Wout': _L1_xattn_in['Wout'], 'L1_xattn_bout': _L1_xattn_in['bout'], 'L1_ffn_w_gate': _L1_ffn_in['w_gate'], 'L1_ffn_w_up': _L1_ffn_in['w_up'], 'L1_ffn_w_down': _L1_ffn_in['w_down'], 'L2_xattn_Wq': _L2_xattn_in['Wq'], 'L2_xattn_Wk': _L2_xattn_in['Wk'], 'L2_xattn_Wv': _L2_xattn_in['Wv'], 'L2_xattn_Wo': _L2_xattn_in['Wo'], 'L2_xattn_gq': _L2_xattn_in['gq'], 'L2_xattn_gk': _L2_xattn_in['gk'], 'L2_ffn_w_router': _L2_ffn_in['w_router'], 'L2_ffn_wg': _L2_ffn_in['wg'], 'L2_ffn_wu': _L2_ffn_in['wu'], 'L2_ffn_wd': _L2_ffn_in['wd'], 'L2_ffn_sw_gate': _L2_ffn_in['sw_gate'], 'L2_ffn_sw_up': _L2_ffn_in['sw_up'], 'L2_ffn_sw_down': _L2_ffn_in['sw_down'], 'L2_ffn_gate_w': _L2_ffn_in['gate_w'], 'L3_xattn_in_proj_w': _L3_xattn_in['in_proj_w'], 'L3_xattn_conv_w': _L3_xattn_in['conv_w'], 'L3_xattn_conv_b': _L3_xattn_in['conv_b'], 'L3_xattn_x_proj_w': _L3_xattn_in['x_proj_w'], 'L3_xattn_dt_proj_w': _L3_xattn_in['dt_proj_w'], 'L3_xattn_dt_proj_b': _L3_xattn_in['dt_proj_b'], 'L3_xattn_A_log': _L3_xattn_in['A_log'], 'L3_xattn_D': _L3_xattn_in['D'], 'L3_ffn_weight': _L3_ffn_in['weight']}

def reference(x, ctx_1024, fside_BxSx2_0, g_xattn, g_ffn, L0_xattn_Wq, L0_xattn_bq, L0_xattn_Wk, L0_xattn_bk, L0_ffn_W_up, L0_ffn_W_down, L0_ffn_W_gate, L0_ffn_W_expert, L1_xattn_Wq, L1_xattn_Wkv, L1_xattn_Wout, L1_xattn_bout, L1_ffn_w_gate, L1_ffn_w_up, L1_ffn_w_down, L2_xattn_Wq, L2_xattn_Wk, L2_xattn_Wv, L2_xattn_Wo, L2_xattn_gq, L2_xattn_gk, L2_ffn_w_router, L2_ffn_wg, L2_ffn_wu, L2_ffn_wd, L2_ffn_sw_gate, L2_ffn_sw_up, L2_ffn_sw_down, L2_ffn_gate_w, L3_xattn_in_proj_w, L3_xattn_conv_w, L3_xattn_conv_b, L3_xattn_x_proj_w, L3_xattn_dt_proj_w, L3_xattn_dt_proj_b, L3_xattn_A_log, L3_xattn_D, L3_ffn_weight):
    import jax
    import jax.numpy as jnp

    def _L0_xattn_ref(teacher_logits, teacher_features, Wq, bq, Wk, bk):
        import jax, jax.numpy as jnp
        import numpy as np
        query = jnp.einsum('bnc,dc->bnd', teacher_features, Wq) + bq
        key = jnp.einsum('bnc,dc->bnd', teacher_features, Wk) + bk
        energy = jnp.einsum('bnd,bmd->bnm', query, key)
        attention = jax.nn.softmax(energy, axis=-1)
        x_m = jnp.einsum('bln,bmn->blm', teacher_logits, attention)
        return x_m

    def _L0_ffn_ref(x, W_up, W_down, W_gate, W_expert):
        import jax, jax.numpy as jnp
        import numpy as np
        DIM = 512
        N_EXPERTS = 8
        TOP_K = 2
        logits = jnp.einsum('bsd,ed->bse', x, W_gate)
        routing_weights, selected_experts = jax.lax.top_k(logits, TOP_K)
        shared_out = jnp.einsum('bsd,od->bso', jax.nn.relu(jnp.einsum('bsd,od->bso', x, W_up)), W_down)
        rw = jax.nn.softmax(routing_weights, axis=-1)
        expert_out = jnp.einsum('bsd,do->bso', x, W_expert)
        moe_out = jnp.sum(rw, axis=-1, keepdims=True) * expert_out
        return shared_out + moe_out

    def _L1_xattn_ref(x, ctx, pos_map, ctx_pos_map, Wq, Wkv, Wout, bout):
        import jax, jax.numpy as jnp
        import numpy as np
        DIM = 512
        CTX_DIM = 256
        N_HEADS = 32
        HEAD_DIM = DIM // N_HEADS
        POS_DIM = 2
        B, N, CTXN = (2, 512, 512)
        ROPE_BASE = 10000.0

        def apply_axial_rope(x, pos):
            b, n, h, d = x.shape
            p = pos.shape[-1]
            dpa = d // p
            half = dpa // 2
            freqs = ROPE_BASE ** (-jnp.arange(half, dtype=x.dtype) / half)
            ang = pos[..., :, None] * freqs
            cos = jnp.cos(ang)[:, :, None, :, :]
            sin = jnp.sin(ang)[:, :, None, :, :]
            xr = x.reshape(b, n, h, p, half, 2)
            x1, x2 = (xr[..., 0], xr[..., 1])
            out = jnp.stack([x1 * cos - x2 * sin, x1 * sin + x2 * cos], axis=-1)
            return out.reshape(b, n, h, d)
        b, n, _ = x.shape
        ctx_n = ctx.shape[1]
        q = (x @ Wq).reshape(b, n, N_HEADS, HEAD_DIM)
        k, v = jnp.split(ctx @ Wkv, 2, axis=-1)
        k = k.reshape(b, ctx_n, N_HEADS, HEAD_DIM)
        v = v.reshape(b, ctx_n, N_HEADS, HEAD_DIM)
        q = apply_axial_rope(q, pos_map)
        k = apply_axial_rope(k, ctx_pos_map)
        scale = 1.0 / np.sqrt(HEAD_DIM).astype(np.float32)
        logits = jnp.einsum('bqhd,bkhd->bhqk', q, k) * scale
        w = jax.nn.softmax(logits, axis=-1)
        attn = jnp.einsum('bhqk,bkhd->bqhd', w, v)
        attn = attn.reshape(b, n, N_HEADS * HEAD_DIM)
        return attn @ Wout + bout

    def _L1_ffn_ref(x, w_gate, w_up, w_down):
        import jax, jax.numpy as jnp
        import numpy as np
        ACT_BITS = 8
        EPS = 1e-05

        def act_quant(x, bits=ACT_BITS):
            qb = float(2 ** (bits - 1))
            scale = qb / jnp.clip(jnp.max(jnp.abs(x), axis=-1, keepdims=True), EPS)
            xq = jnp.clip(jnp.round(x * scale), -qb, qb - 1) / scale
            return x + jax.lax.stop_gradient(xq - x)

        def weight_quant(w):
            scale = 1.0 / jnp.clip(jnp.mean(jnp.abs(w)), EPS)
            wq = jnp.clip(jnp.round(w * scale), -1.0, 1.0) / scale
            return w + jax.lax.stop_gradient(wq - w)

        def fwht(x):
            shape = x.shape
            n = shape[-1]
            x = x.reshape(-1, n)
            h = 1
            while h < n:
                x = x.reshape(-1, n // (2 * h), 2, h)
                a, b = (x[..., 0, :], x[..., 1, :])
                x = jnp.stack([a + b, a - b], axis=-2).reshape(-1, n)
                h *= 2
            return (x * (1.0 / np.sqrt(n)).astype(np.float32)).reshape(shape)

        def bitlinear(x, w):
            return jnp.einsum('bsh,oh->bso', act_quant(x), weight_quant(w))

        def h_bitlinear(x, w):
            return jnp.einsum('bsh,oh->bso', act_quant(fwht(x)), weight_quant(w))
        gate = bitlinear(x, w_gate)
        up = bitlinear(x, w_up)
        intermediate = jax.nn.silu(gate) * up
        return h_bitlinear(intermediate, w_down)

    def _L2_xattn_ref(hidden_states, encoder_hidden_states, Wq, Wk, Wv, Wo, gq, gk):
        import jax, jax.numpy as jnp
        import numpy as np
        EPS = 1e-05

        def rmsnorm(x, g, eps=EPS):
            var = jnp.mean(jnp.square(x), axis=-1, keepdims=True)
            return x * jax.lax.rsqrt(var + eps) * g
        B, Sq, _ = hidden_states.shape
        Skv = encoder_hidden_states.shape[1]
        D = gq.shape[0]
        H = Wq.shape[1] // D
        scale = 1.0 / np.sqrt(D)
        q = (hidden_states @ Wq).reshape(B, Sq, H, D)
        k = (encoder_hidden_states @ Wk).reshape(B, Skv, H, D)
        v = (encoder_hidden_states @ Wv).reshape(B, Skv, H, D)
        q = rmsnorm(q, gq)
        k = rmsnorm(k, gk)
        scores = jnp.einsum('bqhd,bkhd->bhqk', q, k) * scale
        attn = jax.nn.softmax(scores, axis=-1)
        out = jnp.einsum('bhqk,bkhd->bqhd', attn, v)
        out = out.reshape(B, Sq, H * D)
        return out @ Wo

    def _L2_ffn_ref(hidden_states, w_router, wg, wu, wd, sw_gate, sw_up, sw_down, gate_w):
        import jax, jax.numpy as jnp
        import numpy as np
        H = 512
        I = 256
        E = 8
        TOP_K = 2
        IS = 1024
        B, S = (2, 512)

        def _moe_forward(hidden_states, w_router, wg, wu, wd, sw_gate, sw_up, sw_down, gate_w):
            b, s, h = hidden_states.shape
            x = hidden_states.reshape(-1, h)
            t = x.shape[0]
            shared = jax.nn.silu(x @ sw_gate.T) * (x @ sw_up.T) @ sw_down.T
            logits = x @ w_router.T
            probs = jax.nn.softmax(logits.astype(jnp.float32), axis=-1)
            top_v, top_i = jax.lax.top_k(probs, TOP_K)
            top_v = top_v / jnp.sum(top_v, axis=-1, keepdims=True)
            top_v = top_v.astype(probs.dtype)
            combine = jnp.zeros((t, probs.shape[-1]), x.dtype).at[jnp.arange(t)[:, None], top_i].add(top_v)
            g = jax.nn.silu(jnp.einsum('th,eih->tei', x, wg))
            u = jnp.einsum('th,eih->tei', x, wu)
            y = jnp.einsum('tei,ehi->teh', g * u, wd)
            expert_out = jnp.einsum('teh,te->th', y, combine)
            shared = jax.nn.sigmoid(x @ gate_w.T) * shared
            out = expert_out + shared
            return out.reshape(b, s, h)
        return _moe_forward(hidden_states, w_router, wg, wu, wd, sw_gate, sw_up, sw_down, gate_w)

    def _L3_xattn_ref(hidden_states, z, in_proj_w, conv_w, conv_b, x_proj_w, dt_proj_w, dt_proj_b, A_log, D):
        import jax, jax.numpy as jnp
        import numpy as np
        B_, L_, D_MODEL = (4, 512, 256)
        D_STATE, D_CONV, EXPAND = (16, 4, 2)
        D_INNER = EXPAND * D_MODEL
        DT_RANK = (D_MODEL + 15) // 16

        def silu(x):
            return x * jax.nn.sigmoid(x)
        Bsz, L, _ = hidden_states.shape
        d_inner, _, d_conv = conv_w.shape
        dt_rank = dt_proj_w.shape[1]
        d_state = A_log.shape[1]
        x = jnp.einsum('bld,ed->bel', hidden_states, in_proj_w)
        xc = jax.lax.conv_general_dilated(x, conv_w, window_strides=(1,), padding=[(d_conv - 1, 0)], feature_group_count=d_inner, dimension_numbers=('NCH', 'OIH', 'NCH'))
        x = silu(xc + conv_b[None, :, None])
        x_dbl = jnp.einsum('bdl,ed->bel', x, x_proj_w)
        dt_low, Bm, Cm = jnp.split(x_dbl, [dt_rank, dt_rank + d_state], axis=1)
        dt = jnp.einsum('brl,dr->bdl', dt_low, dt_proj_w)
        dt = jax.nn.softplus(dt + dt_proj_b[None, :, None])
        A = -jnp.exp(A_log)
        dt_t = jnp.moveaxis(dt, -1, 0)
        B_t = jnp.moveaxis(Bm, -1, 0)
        C_t = jnp.moveaxis(Cm, -1, 0)
        u_t = jnp.moveaxis(x, -1, 0)

        def step(state, inp):
            d, b, c, u = inp
            dA = jnp.exp(d[..., None] * A)
            state = state * dA + (d * u)[..., None] * b[:, None, :]
            y = jnp.einsum('bdn,bn->bd', state, c)
            return (state, y)
        state0 = jnp.zeros((Bsz, d_inner, d_state), x.dtype)
        _, ys = jax.lax.scan(step, state0, (dt_t, B_t, C_t, u_t))
        y = jnp.moveaxis(ys, 0, 2)
        y = y + D[None, :, None] * x
        y = y * silu(z)
        return jnp.swapaxes(y, 1, 2)

    def _L3_ffn_ref(x, weight):
        import jax, jax.numpy as jnp
        import numpy as np
        BLOCK = 128
        MAXVAL = 448.0

        def _quant_dequant(x_flat):
            xb = x_flat.reshape(-1, BLOCK)
            s = jnp.max(jnp.abs(xb), axis=1, keepdims=True) / MAXVAL
            q = (xb / s).astype(jnp.float8_e4m3fn)
            return (q.astype(jnp.float32) * s).reshape(x_flat.shape)
        B, T, D = x.shape
        x_deq = _quant_dequant(x.reshape(-1)).reshape(B * T, D)
        w_deq = _quant_dequant(weight.reshape(-1)).reshape(weight.shape)
        out = x_deq @ w_deq.T
        return out.reshape(B, T, -1)
    x = x + jnp.tanh(g_xattn[0]) * _L0_xattn_ref(_layernorm(x, axis=-1), ctx_1024, L0_xattn_Wq, L0_xattn_bq, L0_xattn_Wk, L0_xattn_bk)
    x = x + jnp.tanh(g_ffn[0]) * _L0_ffn_ref(_layernorm(x, axis=-1), L0_ffn_W_up, L0_ffn_W_down, L0_ffn_W_gate, L0_ffn_W_expert)
    x = x + jnp.tanh(g_xattn[1]) * _L1_xattn_ref(_layernorm(x, axis=-1), ctx_1024, fside_BxSx2_0, fside_BxSx2_0, L1_xattn_Wq, L1_xattn_Wkv, L1_xattn_Wout, L1_xattn_bout)
    x = x + jnp.tanh(g_ffn[1]) * _L1_ffn_ref(_layernorm(x, axis=-1), L1_ffn_w_gate, L1_ffn_w_up, L1_ffn_w_down)
    x = x + jnp.tanh(g_xattn[2]) * _L2_xattn_ref(_layernorm(x, axis=-1), ctx_1024, L2_xattn_Wq, L2_xattn_Wk, L2_xattn_Wv, L2_xattn_Wo, L2_xattn_gq, L2_xattn_gk)
    x = x + jnp.tanh(g_ffn[2]) * _L2_ffn_ref(_layernorm(x, axis=-1), L2_ffn_w_router, L2_ffn_wg, L2_ffn_wu, L2_ffn_wd, L2_ffn_sw_gate, L2_ffn_sw_up, L2_ffn_sw_down, L2_ffn_gate_w)
    x = x + jnp.tanh(g_xattn[3]) * _L3_xattn_ref(ctx_1024, _layernorm(x, axis=-1), L3_xattn_in_proj_w, L3_xattn_conv_w, L3_xattn_conv_b, L3_xattn_x_proj_w, L3_xattn_dt_proj_w, L3_xattn_dt_proj_b, L3_xattn_A_log, L3_xattn_D)
    x = x + jnp.tanh(g_ffn[3]) * _L3_ffn_ref(_layernorm(x, axis=-1), L3_ffn_weight)
    return x

_drawn_inputs = setup_inputs


def setup_inputs(seed=0):
    import zlib

    import numpy as np

    out = dict(_drawn_inputs(seed))
    spreads = {'L0_xattn_bq': (0.0, 0.1),
     'L0_xattn_bk': (0.0, 2.0),
     'L1_xattn_bout': (0.0, 0.1),
     'L2_xattn_gq': (1.0, 0.6),
     'L2_xattn_gk': (1.0, 0.548),
     'L3_xattn_D': (1.0, 0.6)}
    factors = {'L0_ffn_W_gate': 200.0,
     'L3_xattn_in_proj_w': 5.356,
     'L3_xattn_conv_w': 5.431,
     'L3_xattn_conv_b': 8.0,
     'L3_xattn_x_proj_w': 8.0,
     'L3_xattn_dt_proj_w': 8.0,
     'L3_xattn_dt_proj_b': 8.0,
     'L3_xattn_A_log': 8.0,
     'g_ffn': 43.84,
     'L3_ffn_weight': 8.0}
    for name, (base, spread) in spreads.items():
        noise = np.random.default_rng([zlib.crc32(name.encode()), seed]).standard_normal(out[name].shape)
        drawn = base * np.exp(spread * noise) if base else spread * noise
        out[name] = jnp.asarray(drawn.astype(out[name].dtype))
    for name, factor in factors.items():
        out[name] = (out[name] * factor).astype(out[name].dtype)
    return out
```

```python
import numpy as np
import concourse.bass as bass
from concourse import mybir
from contextlib import ExitStack

F32 = mybir.dt.float32
F32R = mybir.dt.float32r
BF16 = mybir.dt.bfloat16
I32 = mybir.dt.int32
ALU = mybir.AluOpType
ACT = mybir.ActivationFunctionType
AX = mybir.AxisListType

P = 128
NB, S, D, C = 4, 512, 512, 256
ST = S // P
DC = D // P
CC = C // P
LN_EPS = 1e-5


class Ring:

    def __init__(self, sem, name, banks, jobs):
        self.banks, self.jobs = banks, [n for n, _ in jobs]
        self.who = [w for _, w in jobs]
        assert len(jobs) % len(banks) == 0, (name, len(jobs))
        self.index = {n: k for k, n in enumerate(self.jobs)}
        assert len(self.index) == len(jobs)
        self.filled_sem = sem(name + "_filled")
        self.per_body = sum(w is not None for w in self.who)
        self.drained_sem = {w: sem(f"{name}_drained_{w}") for w in set(self.who) - {None}}

    def bank(self, job):
        return self.banks[self.index[job] % len(self.banks)]

    def _rank(self, k, who=None):
        return sum(w is not None and (who is None or w == who) for w in self.who[:k + 1])

    def credit(self, eng, who):
        eng.sem_inc(self.drained_sem[who], self.who.count(who))

    def wait_for(self, eng, i, free=None, drained=()):
        least = {}
        if free is not None:
            m, per = self.index[free] - len(self.banks), 1
            while m < 0 or self.who[m] is None:
                if m < 0:
                    m, per = m + len(self.jobs), per - 1
                else:
                    m -= len(self.banks)
            w = self.who[m]
            least[w] = per * self.who.count(w) + self._rank(m, w)
        for job in drained:
            k = self.index[job]
            w = self.who[k]
            least[w] = max(least.get(w, 0), self.who.count(w) + self._rank(k, w))
        for w, n in least.items():
            eng.wait_ge(self.drained_sem[w], i * self.who.count(w) + n)

    def wait_filled(self, eng, i, job):
        eng.wait_ge(self.filled_sem, i * self.per_body + self._rank(self.index[job]))

    def skip_fill(self, pe, i, jobs):
        before = i * self.per_body + self._rank(self.index[jobs[0]]) - 1
        if not (isinstance(before, int) and before == 0):
            pe.wait_ge(self.filled_sem, before)
        pe.sem_inc(self.filled_sem, sum(self.who[self.index[j]] is not None for j in jobs))

    def skip_drain(self, eng, i, who, jobs):
        mine = [j for j in jobs if self.who[self.index[j]] == who]
        if mine:
            n = self.who.count(who)
            eng.wait_ge(self.drained_sem[who], (i + 1) * n + self._rank(self.index[mine[0]], who) - 1)
            eng.sem_inc(self.drained_sem[who], len(mine))

    def fill(self, ins):
        ins.then_inc(self.filled_sem, 1)

    def drain(self, ins, job, banks=1):
        ins.then_inc(self.drained_sem[self.who[self.index[job]]], banks)


class Steps:

    def __init__(self, sem, per):
        self.sem, self.per, self.n, self.i = sem, per, 0, 0

    def begin(self, i):
        self.i, self.n = i, 0

    def end(self):
        assert self.n == self.per, f"{self.sem}: {self.n} signals in a body, {self.per} stated"

    def inc(self, ins):
        ins.then_inc(self.sem, 1)
        self.n += 1

    def wait(self, eng, n=None):
        eng.wait_ge(self.sem, self.i * self.per + (self.n if n is None else n))


def transpose_group(pe, bank, tiles, ident):
    for k, tile in enumerate(tiles):
        last = pe.transpose(bank[:, k * P:(k + 1) * P], tile, ident)
    return last


def product(pe, out, pairs):
    for k, (lhsT, rhs) in enumerate(pairs):
        last = pe.matmul(out, lhsT, rhs, start=(k == 0), stop=(k == len(pairs) - 1))
    return last


def split_product(pe, out, pairs):
    three = [(lhsT[m], rhs[n]) for lhsT, rhs in pairs for m, n in ((0, 0), (0, 1), (1, 0))]
    return product(pe, out, three)


class LayerNorm:
    DVE_STEPS = 4 + 2 + 2 + 1

    def __init__(self, g, sem):
        self.g = g
        self.steps = Steps(sem("ln_steps"), self.DVE_STEPS)
        self.var_ready, self.rstd_ready, self.xn_ready = sem("ln_var_ready"), sem("ln_rstd_ready"), sem("ln_xn_ready")

    def vector(self, dve, i, batch, xn_free):
        g, st = self.g, self.steps
        st.begin(i)
        stats, w = g["ln_stats"], g["ln_work"]
        for s in range(ST):
            st.inc(dve.bn_stats(stats[:, s, :], g["x"][:, batch * ST + s, :]))
        st.wait(dve)
        st.inc(dve.tensor_tensor(w[:, 0, :], stats[:, :, 1], stats[:, :, 4], ALU.subtract))
        st.inc(dve.tensor_tensor(w[:, 1, :], stats[:, :, 2], stats[:, :, 5], ALU.add))
        st.wait(dve)
        st.inc(dve.scalar_tensor_tensor(w[:, 2, :], w[:, 0, :], float(D) / 4, w[:, 0, :], ALU.mult, ALU.mult))
        st.inc(dve.tensor_tensor(w[:, 3, :], stats[:, :, 1], stats[:, :, 4], ALU.add))
        st.wait(dve)
        st.inc(dve.tensor_tensor(w[:, 4, :], w[:, 2, :], w[:, 1, :], ALU.add))
        st.wait(dve)
        dve.tensor_scalar(w[:, 5, :], w[:, 4, :], 1.0 / D, LN_EPS, ALU.mult, ALU.add).then_inc(self.var_ready, 1)
        dve.tensor_scalar(w[:, 6, :], w[:, 3, :], 0.5, None, ALU.mult).then_inc(self.var_ready, 1)
        xn_free()
        dve.wait_ge(self.var_ready, i * 2 + 2)
        dve.wait_ge(self.rstd_ready, i + 1)
        for s in range(ST):
            dve.tensor_scalar(g["xn"][:, s, :], g["x"][:, batch * ST + s, :], w[:, 6, s:s + 1],
                              w[:, 7, s:s + 1], ALU.subtract, ALU.mult).then_inc(self.xn_ready, 1)
        st.end()

    def pool(self, pool, i):
        w = self.g["ln_work"]
        pool.wait_ge(self.var_ready, i * 2 + 2)
        pool.tensor_tensor(w[:, 7, :], w[:, 5, :], self.g["minus_half"][:, 0:ST], ALU.pow).then_inc(self.rstd_ready, 1)

    def credit(self, dve):
        dve.sem_inc(self.xn_ready, 1)

    def wait_xn(self, pe, i):
        pe.wait_ge(self.xn_ready, i * ST + 1)


def xt_jobs():
    return [(f"xt{c}", "act" if c % 2 else "dve") for c in range(DC)]


def xt_fill(pe, g, ln, ring, i):
    ln.wait_xn(pe, i)
    for c in range(DC):
        ring.wait_for(pe, i, free=f"xt{c}")
        ring.fill(transpose_group(pe, g["psum"][:, ring.bank(f"xt{c}"), :],
                                  [g["xn"][:, s, c * P:(c + 1) * P] for s in range(ST)], g["ident"][:]))


def xt_drain(eng, who, g, ring, i, xt):
    for c in range(DC):
        if ring.who[ring.index[f"xt{c}"]] == who:
            ring.wait_filled(eng, i, f"xt{c}")
            copy(eng, who, ring, f"xt{c}", xt[:, c, :], g["psum"][:, ring.bank(f"xt{c}"), :])


def copy(eng, who, ring, job, out, in_):
    ring.drain(eng.tensor_copy(out, in_) if who == "dve" else eng.activation(out, in_, ACT.Copy), job)


def residual(dve, ring, i, job, g, tile, scale):
    ring.wait_filled(dve, i, job)
    ring.drain(dve.scalar_tensor_tensor(g["x"][:, tile, :], g["psum"][:, ring.bank(job), :], scale,
                                        g["x"][:, tile, :], ALU.mult, ALU.add), job)


class Phase:

    def __init__(self, nc, tag):
        self.nc, self.tag, self.stack, self.sems = nc, tag, ExitStack(), []

    def __enter__(self):
        self.stack.__enter__()
        return self

    def __exit__(self, *a):
        done = self.stack.__exit__(*a)
        self.nc.clear_and_free_semaphores(self.sems)
        self.nc.all_engine_barrier()
        return done

    def sb(self, name, shape, dt=F32):
        return self.stack.enter_context(self.nc.sbuf_tensor(f"{self.tag}_{name}", shape, dt))

    def sem(self, name):
        self.sems.append(self.nc.alloc_semaphore(f"{self.tag}_{name}"))
        return self.sems[-1]

    def block(self):
        return self.stack.enter_context(self.nc.Block())


def setup(nc, g, a):
    with Phase(nc, "setup") as ph:
        sem, sb = ph.sem, ph.sb
        loaded = sem("loaded")
        ident_done, angle_done, steps_sem, tanh_done = [sem(n) for n in (
            "ident_done", "angle_done", "steps", "tanh_done")]
        g_raw = sb("g_raw", [P, 8])
        pos = sb("pos", [P, NB * ST, 2])
        ang = sb("ang", [P, 2, NB * ST, 2, 4])
        turns = sb("turns", [P, 2, NB * ST, 2, 4])
        ln = LayerNorm(g, sem)
        blk = ph.block()

        @blk.sync
        def _(sp):
            sp.dma_start(g["x"][:], a["x"].rearrange("(t p) d -> p t d", p=P)).then_inc(loaded, 16)
            sp.dma_start(g_raw[:, 0:4], a["g_xattn"].partition_broadcast(P)).then_inc(loaded, 16)
            sp.dma_start(g_raw[:, 4:8], a["g_ffn"].partition_broadcast(P)).then_inc(loaded, 16)
            sp.dma_start(pos[:], a["pos"].rearrange("(t p) k -> p t k", p=P)).then_inc(loaded, 16)

        @blk.gpsimd
        def _(pool):
            pool.memset(g["ident"][:], 0.0).then_inc(ident_done, 1)
            pool.memset(g["ident_bf"][:], 0.0).then_inc(ident_done, 1)
            pool.memset(g["minus_half"][:], -0.5).then_inc(ident_done, 1)
            pool.memset(g["inv_p"][:], 1.0 / P).then_inc(ident_done, 1)
            pool.memset(g["eps"][:], LN_EPS).then_inc(ident_done, 1)
            pool.wait_ge(ident_done, 5)
            for m in (g["ident"], g["ident_bf"]):
                pool.affine_select(out=m[:], in_=m[:], compare_op=ALU.not_equal, fill=1.0, base=0,
                                   pattern=[[-1, P]], channel_multiplier=1).then_inc(ident_done, 1)
            ln.pool(pool, 0)

        @blk.vector
        def _(dve):
            st = Steps(steps_sem, 11)
            st.begin(0)
            dve.wait_ge(loaded, 64)
            for j in range(4):
                st.inc(dve.tensor_scalar(ang[:, 1, :, :, j], pos[:], 10.0 ** -j, None, ALU.mult))
            st.wait(dve)
            st.inc(dve.tensor_scalar(ang[:, 0], ang[:, 1], float(np.pi / 2), None, ALU.add))
            st.wait(dve)
            st.inc(dve.tensor_scalar(turns[:], ang[:], float(1 / (2 * np.pi)), ROUND, ALU.mult, ALU.add))
            st.wait(dve)
            st.inc(dve.tensor_scalar(turns[:], turns[:], ROUND, None, ALU.subtract))
            for part in (-6.28125, -(2 * np.pi - 6.28125)):
                st.wait(dve)
                st.inc(dve.scalar_tensor_tensor(ang[:], turns[:], float(part), ang[:], ALU.mult, ALU.add))
            st.wait(dve)
            st.inc(dve.tensor_scalar(ang[:], ang[:], 3.1415925, -3.1415925, ALU.min, ALU.max))
            st.inc(dve.memset(g["ones"][:], 1.0))
            st.end()
            ln.vector(dve, 0, 0, lambda: None)

        @blk.scalar
        def _(act):
            act.wait_ge(steps_sem, 11)
            act.activation(g["rope"][:], ang[:], ACT.Sin).then_inc(angle_done, 1)
            act.wait_ge(loaded, 64)
            act.activation(g["gate"][:], g_raw[:], ACT.Tanh).then_inc(tanh_done, 1)


ROUND = 12582912.0


def l0_xattn(nc, g, a):
    with Phase(nc, "l0x") as ph:
        sem, sb = ph.sem, ph.sb
        wq, wk = sb("wq", [P, CC, P]), sb("wk", [P, CC, P])
        bias = sb("bias", [P, 2])
        ctx_t = sb("ctx_t", [P, 2, CC, S])
        xt, qt, kt = sb("xt", [P, DC, S]), sb("qt", [P, S]), sb("kt", [P, S])
        probs, probs_t = sb("probs", [P, ST, S]), sb("probs_t", [P, ST, S])
        neg_max, total, inv = sb("neg_max", [P, ST]), sb("total", [P, ST]), sb("inv", [P, ST])
        ring = Ring(sem, "l0x", range(6), xt_jobs() + [("q", "act"), ("k", "dve")]
                    + [(f"e{m}", "act") for m in range(ST)]
                    + [(f"pt{n}", "dve" if n % 2 else "act") for n in range(ST)]
                    + [(f"out{l}", "dve") for l in range(ST)])
        weights_in, ctx_in, max_ready, inv_ready, probs_ready = [sem(n) for n in (
            "weights_in", "ctx_in", "max_ready", "inv_ready", "probs_ready")]
        ln = LayerNorm(g, sem)
        blk = ph.block()

        def bank(job):
            return g["psum"][:, ring.bank(job), :]

        @blk.sync
        def _(sp):
            sp.dma_start(wq[:], a["l0_wq"].rearrange("(c p) d -> p c d", p=P)).then_inc(weights_in, 16)
            sp.dma_start(wk[:], a["l0_wk"].rearrange("(c p) d -> p c d", p=P)).then_inc(weights_in, 16)
            sp.dma_start(bias[:, 0:1], a["l0_bq"].rearrange("(p o) -> p o", o=1)).then_inc(weights_in, 16)
            sp.dma_start(bias[:, 1:2], a["l0_bk"].rearrange("(p o) -> p o", o=1)).then_inc(weights_in, 16)
            for b in range(NB):
                if b >= 1:
                    sp.wait_ge(ctx_in, b * 16)
                if b >= 2:
                    ring.wait_filled(sp, b - 2, "k")
                sp.dma_start(ctx_t[:, b % 2], a["ctx_t"][:, b * S:(b + 1) * S].rearrange("(c p) n -> p c n", p=P)
                             ).then_inc(ctx_in, 16)

        @blk.tensor
        def _(pe):
            pe.wait_ge(weights_in, 64)
            with pe.Fori(0, NB) as i:
                xt_fill(pe, g, ln, ring, i)
                pe.wait_ge(ctx_in, (i + 1) * 16)
                for job, w in (("q", wq), ("k", wk)):
                    ring.wait_for(pe, i, free=job)
                    ring.fill(product(pe, bank(job), [(w[:, c, :], ctx_t[:, i & 1, c, :]) for c in range(CC)]))
                for m in range(ST):
                    ring.wait_for(pe, i, free=f"e{m}", drained=["q", "k"])
                    ring.fill(product(pe, bank(f"e{m}"), [(qt[:, m * P:(m + 1) * P], kt[:])]))
                pe.wait_ge(probs_ready, (i + 1) * ST)
                for n in range(ST):
                    ring.wait_for(pe, i, free=f"pt{n}")
                    ring.fill(transpose_group(pe, bank(f"pt{n}"), [probs[:, m, n * P:(n + 1) * P] for m in range(ST)],
                                              g["ident"][:]))
                for l in range(ST):
                    ring.wait_for(pe, i, free=f"out{l}", drained=["pt2", "pt3"])
                    ring.fill(product(pe, bank(f"out{l}"), [(xt[:, n, l * P:(l + 1) * P], probs_t[:, n, :])
                                                            for n in range(ST)]))

        @blk.scalar
        def _(act):
            act.wait_ge(weights_in, 64)
            ring.credit(act, "act")
            with act.Fori(0, NB) as i:
                xt_drain(act, "act", g, ring, i, xt)
                ring.wait_filled(act, i, "q")
                ring.drain(act.activation(qt[:], bank("q"), ACT.Identity, bias=bias[:, 0:1]), "q")
                for m in range(ST):
                    act.wait_ge(max_ready, i * ST + m + 1)
                    ring.drain(act.activation(probs[:, m, :], bank(f"e{m}"), ACT.Exp, bias=neg_max[:, m:m + 1],
                                              accum_out=total[:, m:m + 1]), f"e{m}")
                for n in (0, 2):
                    ring.wait_filled(act, i, f"pt{n}")
                    copy(act, "act", ring, f"pt{n}", probs_t[:, n, :], bank(f"pt{n}"))

        @blk.vector
        def _(dve):
            dve.wait_ge(weights_in, 64)
            ring.credit(dve, "dve")
            ln.credit(dve)
            with dve.Fori(0, NB) as i:
                xt_drain(dve, "dve", g, ring, i, xt)
                ring.wait_filled(dve, i, "k")
                ring.drain(dve.tensor_scalar(kt[:], bank("k"), bias[:, 1:2], None, ALU.add), "k")
                for m in range(ST):
                    ring.wait_filled(dve, i, f"e{m}")
                    dve.tensor_reduce(neg_max[:, m:m + 1], bank(f"e{m}"), AX.X, ALU.max,
                                      negate=True).then_inc(max_ready, 1)
                for m in range(ST):
                    ring.wait_for(dve, i, drained=[f"e{m}"])
                    dve.reciprocal(inv[:, m:m + 1], total[:, m:m + 1]).then_inc(inv_ready, 1)
                    dve.wait_ge(inv_ready, i * ST + m + 1)
                    dve.tensor_scalar(probs[:, m, :], probs[:, m, :], inv[:, m:m + 1], None,
                                      ALU.mult).then_inc(probs_ready, 1)
                for n in (1, 3):
                    ring.wait_filled(dve, i, f"pt{n}")
                    copy(dve, "dve", ring, f"pt{n}", probs_t[:, n, :], bank(f"pt{n}"))
                dve.wait_ge(ring.drained_sem["dve"], (i + 1) * ring.who.count("dve"))
                ln.vector(dve, i, (i + 1) & 3, lambda: ring.wait_filled(dve, i, "xt3"))
                for l in range(ST):
                    residual(dve, ring, i, f"out{l}", g, i * ST + l, g["gate"][:, 0:1])

        @blk.gpsimd
        def _(pool):
            with pool.Fori(0, NB) as i:
                ln.pool(pool, i)


def l0_ffn(nc, g, a):
    with Phase(nc, "l0f") as ph:
        sem, sb = ph.sem, ph.sb
        raw = [sb(n, [P, DC, D]) for n in ("up", "down", "expert")]
        up, down, expert = split_weights = [[sb(f"{n}_{part}", [P, DC, D], F32R) for part in ("hi", "lo")]
                                            for n in ("up", "down", "expert")]
        router = sb("router", [P, DC, 8])
        xt = sb("xt", [P, DC, S])
        xt_parts, ht = [[sb(f"{n}_{part}", [P, DC, S], F32R) for part in ("hi", "lo")] for n in ("xt", "ht")]
        top = sb("top", [P, ST, 8])
        small = sb("small", [P, 8, ST])
        ring = Ring(sem, "l0f", range(6), [(f"xt{c}", "dve") for c in range(DC)] + [("router", "dve")]
                    + [(f"h{m}", "dve") for m in range(DC)]
                    + [(f"{k}{t}", "dve") for t in range(ST) for k in ("sh", "ex")] + [("spare", None)])
        weights_in, top_ready, exp_ready, dve_steps, w_hi, w_lo, x_hi, h_hi = [sem(n) for n in (
            "weights_in", "top_ready", "exp_ready", "dve_steps", "w_hi", "w_lo", "x_hi", "h_hi")]
        ln = LayerNorm(g, sem)
        blk = ph.block()

        def bank(job):
            return g["psum"][:, ring.bank(job), :]

        @blk.sync
        def _(sp):
            for w, name in ((router, "l0_router"), (raw[0], "l0_up"), (raw[1], "l0_down"), (raw[2], "l0_expert")):
                sp.dma_start(w[:], a[name].rearrange("(c p) d -> p c d", p=P)).then_inc(weights_in, 16)

        @blk.tensor
        def _(pe):
            pe.wait_ge(weights_in, 64)
            with pe.Fori(0, NB) as i:
                xt_fill(pe, g, ln, ring, i)
                ring.wait_for(pe, i, free="router", drained=["xt2", "xt3"])
                for t in range(ST):
                    last = product(pe, bank("router")[:, t * 8:t * 8 + 8],
                                   [(xt[:, c, t * P:(t + 1) * P], router[:, c, :]) for c in range(DC)])
                ring.fill(last)
                pe.wait_ge(w_lo, 3)
                for m in range(DC):
                    ring.wait_for(pe, i, free=f"h{m}")
                    ring.fill(split_product(pe, bank(f"h{m}"), [([w[:, c, m * P:(m + 1) * P] for w in up],
                                                                 [x[:, c, :] for x in xt_parts]) for c in range(DC)]))
                for t in range(ST):
                    for job, act_t, w in ((f"sh{t}", ht, down), (f"ex{t}", xt_parts, expert)):
                        ring.wait_for(pe, i, free=job, drained=[f"h{DC - 1}"])
                        ring.fill(split_product(pe, bank(job), [([m[:, c, t * P:(t + 1) * P] for m in act_t],
                                                                 [m[:, c, :] for m in w]) for c in range(DC)]))

        @blk.scalar
        def _(act):
            act.wait_ge(weights_in, 64)
            for whole, (hi, _) in zip(raw, split_weights):
                act.activation(hi[:], whole[:], ACT.Copy).then_inc(w_hi, 1)
            with act.Fori(0, NB) as i:
                for c in range(DC):
                    ring.wait_filled(act, i, f"xt{c}")
                    act.activation(xt[:, c, :], bank(f"xt{c}"), ACT.Copy).then_inc(x_hi, 1)
                    act.activation(xt_parts[0][:, c, :], bank(f"xt{c}"), ACT.Copy).then_inc(x_hi, 1)
                for m in range(DC):
                    ring.wait_filled(act, i, f"h{m}")
                    act.activation(ht[0][:, m, :], bank(f"h{m}"), ACT.Relu).then_inc(h_hi, 1)
                act.wait_ge(top_ready, i + 1)
                act.activation(small[:, 1, :], small[:, 0, :], ACT.Exp).then_inc(exp_ready, 1)

        @blk.vector
        def _(dve):
            st = Steps(dve_steps, ST + 5)
            ring.credit(dve, "dve")
            ln.credit(dve)
            with dve.Fori(0, NB) as i:
                st.begin(i)
                for c in range(DC):
                    dve.wait_ge(x_hi, (i * DC + c + 1) * 2)
                    ring.drain(dve.tensor_tensor(xt_parts[1][:, c, :], bank(f"xt{c}"), xt_parts[0][:, c, :].bitcast(F32),
                                                 ALU.subtract), f"xt{c}")
                ring.wait_filled(dve, i, "router")
                st.inc(dve.memset(small[:, 7, :], 0.0))
                for t in range(ST):
                    ins = dve.max(top[:, t, :], bank("router")[:, t * 8:t * 8 + 8])
                    if t == ST - 1:
                        ring.drain(ins, "router")
                    else:
                        st.inc(ins)
                st.wait(dve)
                ring.wait_for(dve, i, drained=["router"])
                dve.tensor_tensor(small[:, 0, :], top[:, :, 1], top[:, :, 0], ALU.subtract).then_inc(top_ready, 1)
                for m in range(DC):
                    dve.wait_ge(h_hi, i * DC + m + 1)
                    ring.drain(dve.scalar_tensor_tensor(ht[1][:, m, :], bank(f"h{m}"), 0.0, ht[0][:, m, :].bitcast(F32),
                                                        ALU.max, ALU.subtract), f"h{m}")
                dve.wait_ge(ring.drained_sem["dve"], (i + 1) * ring.who.count("dve"))
                ln.vector(dve, i, (i + 1) & 3, lambda: ring.wait_filled(dve, i, "xt3"))
                dve.wait_ge(exp_ready, i + 1)
                st.inc(dve.tensor_scalar(small[:, 2, :], small[:, 1, :], 1.0, None, ALU.add))
                st.wait(dve)
                st.inc(dve.reciprocal(small[:, 3, :], small[:, 2, :]))
                st.wait(dve)
                st.inc(dve.tensor_tensor(small[:, 4, :], small[:, 1, :], small[:, 3, :], ALU.mult))
                st.wait(dve)
                st.inc(dve.tensor_tensor(small[:, 5, :], small[:, 3, :], small[:, 4, :], ALU.add))
                st.wait(dve)
                st.inc(dve.tensor_scalar(small[:, 6, :], small[:, 5, :], g["gate"][:, 4:5], None, ALU.mult))
                st.wait(dve)
                for t in range(ST):
                    residual(dve, ring, i, f"sh{t}", g, i * ST + t, g["gate"][:, 4:5])
                    ring.wait_for(dve, i, drained=[f"sh{t}"])
                    residual(dve, ring, i, f"ex{t}", g, i * ST + t, small[:, 6, t:t + 1])
                st.end()

        @blk.gpsimd
        def _(pool):
            for k, (whole, (hi, lo)) in enumerate(zip(raw, split_weights)):
                pool.wait_ge(w_hi, k + 1)
                pool.tensor_tensor(lo[:], whole[:], hi[:].bitcast(F32), ALU.subtract).then_inc(w_lo, 1)
            with pool.Fori(0, NB) as i:
                ln.pool(pool, i)


H1, HD = 32, 16
HG = 4
NG = H1 // HG
VW = HD + 1
SLOTS = 8
SETS = 3


def rope_tile(eng, st, g, raw, prod, rot, split, tile):
    x1, x2 = [raw[:, k, :].rearrange("p (h m) -> p h m", m=HD // 2) for k in range(2)]
    cos, sin = [g["rope"][:, k, tile].rearrange("p a j -> p (a j)").unsqueeze(1).to_broadcast([P, H1, HD // 2])
                for k in range(2)]
    pr = [prod[:, k, :].rearrange("p (h m) -> p h m", m=HD // 2) for k in range(4)]
    for out, x, f in ((pr[0], x1, cos), (pr[1], x2, sin), (pr[2], x1, sin), (pr[3], x2, cos)):
        st.inc(eng.tensor_tensor(out, x, f, ALU.mult))
    st.wait(eng)
    half = HD // 2
    st.inc(eng.tensor_tensor(rot[:, :, 0:half], pr[0], pr[1], ALU.subtract))
    st.inc(eng.tensor_tensor(rot[:, :, half:HD], pr[2], pr[3], ALU.add))
    st.wait(eng)
    one = g["ones"][:, 0:1].unsqueeze(2).to_broadcast([P, H1, HD])
    st.inc(eng.tensor_tensor(split[:, :, 0:HD].bitcast(F32R), rot[:], one, ALU.mult))
    st.wait(eng)
    return eng.tensor_tensor(split[:, :, HD:2 * HD], rot[:], split[:, :, 0:HD], ALU.subtract)


ROPE_STEPS = 7


def l1_xattn(nc, g, a):
    with Phase(nc, "l1x") as ph:
        sem, sb = ph.sem, ph.sb
        wq, wkv, wout = sb("wq", [P, DC, D]), sb("wkv", [P, CC, 2 * D]), sb("wout", [P, DC, D])
        bout = sb("bout", [1, D])
        ctx_t = sb("ctx_t", [P, CC, S])
        xt = sb("xt", [P, DC, S])
        q_raw, k_raw = [sb(n, [P, 2, 2, D // 2]) for n in ("q_raw", "k_raw")]
        q_prod, k_prod = [sb(n, [P, 4, D // 2]) for n in ("q_prod", "k_prod")]
        q_rot, k_rot = [sb(n, [P, H1, HD]) for n in ("q_rot", "k_rot")]
        q_split, k_split = [sb(n, [P, ST, H1, 2 * HD]) for n in ("q_split", "k_split")]
        stage = sb("stage", [P, SLOTS - 4, S])
        slots = [stage[:, n, :] for n in range(SLOTS - 4)] + [m[:, n].rearrange("p a b -> p (a b)")
                                                              for m in (k_raw, q_raw) for n in range(2)]
        qs, ks = [[sb(f"{n}{k}", [P, HG, S], F32R) for k in range(SETS)] for n in ("qs", "ks")]
        v = sb("v", [P, ST, H1 * VW + 2 * HD - VW])
        probs = k_split[:].rearrange("p a h r -> p (a h r)").rearrange("p (b j n) -> p b j n", b=2, j=HG)
        o_sb = sb("o_sb", [P, S])
        attn = q_split[:].rearrange("p a h r -> p (a h r)")[:, 0:ST * D].rearrange("p (t n) -> p t n", t=ST)
        inv = sb("inv", [P, 2, ST, HG])
        mx, mx_split = sb("mx", [P, 2, HG, ST]), sb("mx_split", [P, 2, 2 * HG * ST])
        rows = sb("rows", [2 * HG * ST, 2, P])
        heads_dram = nc.dram_tensor("l1x_heads_dram", [2, NG, P, S], F32).ap()
        rows_dram = nc.dram_tensor("l1x_rows_dram", [NG, 2 * HG * ST, P], F32).ap()

        main = Ring(sem, "l1x", (0, 1), xt_jobs()
                    + [(f"{n}{s}", "act") for n in "kqv" for s in range(ST)]
                    + [(f"t{n}{gr}", w) for gr in range(NG) for n, w in (("k", "act"), ("q", "dve"))]
                    + l1_main_order())
        score = Ring(sem, "l1s", (2, 3, 4, 5), [(f"s{gr}_{kt}_{j}", "act") for gr in range(NG)
                                                for kt in range(ST) for j in range(HG)])
        outr = Ring(sem, "l1o", (6, 7), [(f"o{gr}", "act") for gr in range(NG)])
        (weights_in, ctx_in, k_rope, q_rope, k_steps, q_steps, mx_hi, mx_lo, row_out, row_in, inv_done,
         ones_done) = [sem(n) for n in ("weights_in", "ctx_in", "k_rope", "q_rope", "k_steps", "q_steps",
                                        "mx_hi", "mx_lo", "row_out", "row_in", "inv_done", "ones_done")]
        staged_out = [sem(f"staged_out{k}") for k in range(SLOTS)]
        set_in = [sem(f"set_in{k}") for k in range(SETS)]
        per_set = [len(range(k, NG, SETS)) for k in range(SETS)]
        ln = LayerNorm(g, sem)
        blk = ph.block()

        def bank(job, ring=main):
            return g["psum"][:, ring.bank(job), :]

        ctx_src = a["ctx_t"].rearrange("(c p) n -> p c n", p=P)

        def wait_set(eng, i, gr):
            k = gr % SETS
            eng.wait_ge(set_in[k], (i * per_set[k] + gr // SETS + 1) * 80)

        @blk.sync
        def _(sp):
            for w, name in ((wkv, "l1_wkv"), (wq, "l1_wq"), (wout, "l1_wout")):
                sp.dma_start(w[:], a[name].rearrange("(c p) d -> p c d", p=P)).then_inc(weights_in, 16)
            sp.dma_start(bout[:], a["l1_bout"].rearrange("(o n) -> o n", o=1)).then_inc(weights_in, 16)
            sp.dma_start(ctx_t[:], ctx_src[:, :, 0:S]).then_inc(ctx_in, 16)
            for done in staged_out:
                sp.sem_inc(done, 1)
            with sp.Fori(0, NB) as i:
                def load(gr):
                    k = gr % SETS
                    if gr >= SETS:
                        score.wait_filled(sp, i, f"s{gr - SETS}_{ST - 1}_{HG - 1}")
                    for m, slot in ((1, (2 * gr) % SLOTS), (0, (2 * gr + 1) % SLOTS)):
                        sp.wait_ge(staged_out[slot], ((i * (2 * NG // SLOTS) + 2 * gr // SLOTS) + 1) * 16 + 1)
                    q, kk = [heads_dram[m, gr].rearrange("(j r) n -> r j n", j=HG) for m in range(2)]
                    for dst, lo, src in ((qs, 0, q), (qs, 32, q[HD:2 * HD]), (qs, 48, q[0:HD]),
                                         (ks, 0, kk), (ks, 32, kk)):
                        sp.dma_start(dst[k][lo:lo + src.shape[0], :, :].bitcast(F32), src).then_inc(set_in[k], 16)

                def rows_in(gr):
                    main.wait_for(sp, i, drained=[f"nm{gr}"])
                    sp.dma_start(rows_dram[gr], rows[:, gr % 2, :]).then_inc(row_out, 16)
                    sp.wait_ge(row_out, (i * NG + gr + 1) * 16)
                    sp.dma_start(qs[gr % SETS][64:66, :, :].bitcast(F32),
                                 rows_dram[gr].rearrange("(a j t) n -> a j (t n)", a=2, j=HG)).then_inc(row_in, 16)

                for gr in range(NG):
                    for n, m, slot in (("k", 1, (2 * gr) % SLOTS), ("q", 0, (2 * gr + 1) % SLOTS)):
                        main.wait_for(sp, i, drained=[f"t{n}{gr}"])
                        sp.dma_start(heads_dram[m, gr], slots[slot]).then_inc(staged_out[slot], 16)
                    if 1 <= gr <= SETS:
                        load(gr - 1)
                for gr in range(NG):
                    if gr >= 2 and gr + 1 < NG:
                        load(gr + 1)
                    rows_in(gr)
            sp.wait_ge(ctx_in, (NB + 1) * 16)

        @blk.tensor
        def _(pe):
            pe.wait_ge(weights_in, 64)
            pe.wait_ge(ones_done, 3 * 2 * SETS + 1)
            with pe.Fori(0, NB) as i:
                def max_job(h, t):
                    gr, j = divmod(h, HG)
                    k = gr % SETS
                    if j == 0 and t == 0:
                        wait_set(pe, i, gr)
                    job = f"m{h}_{t}"
                    main.wait_for(pe, i, free=job)
                    main.fill(pe.matmul(bank(job), qs[k][0:64, j, t * P:(t + 1) * P], ks[k][0:64, j, :],
                                        start=True, stop=True))

                def rows_job(gr):
                    pe.wait_ge(mx_lo, i * NG + gr + 1)
                    main.wait_for(pe, i, free=f"nm{gr}")
                    main.fill(pe.transpose(bank(f"nm{gr}")[0:2 * HG * ST, 0:P], mx_split[:, gr % 2, :],
                                           g["ident"][:]))

                def score_job(gr, kt, j):
                    if kt == 0 and j == 0:
                        pe.wait_ge(row_in, (i * NG + gr + 1) * 16)
                    job = f"s{gr}_{kt}_{j}"
                    score.wait_for(pe, i, free=job)
                    score.fill(pe.matmul(bank(job, score), ks[gr % SETS][:, j, kt * P:(kt + 1) * P],
                                         qs[gr % SETS][:, j, :], start=True, stop=True))

                def value_jobs(gr, kt):
                    score.wait_for(pe, i, drained=[f"s{gr}_{kt}_{HG - 1}"])
                    if kt == 0:
                        outr.wait_for(pe, i, free=f"o{gr}")
                    for j in range(HG):
                        h = gr * HG + j
                        last = pe.matmul(bank(f"o{gr}", outr)[32 * j:32 * j + 32, :], v[:, kt, h * VW:h * VW + 2 * HD],
                                         probs[:, kt % 2, j, :], start=(kt == 0), stop=(kt == ST - 1),
                                         tile_position=(0, 32 * j))
                    if kt == ST - 1:
                        outr.fill(last)

                def turn_out(gr):
                    outr.wait_for(pe, i, drained=[f"o{gr}"])
                    main.wait_for(pe, i, free=f"ot{gr}")
                    main.fill(transpose_group(pe, bank(f"ot{gr}"), [o_sb[:, t * P:(t + 1) * P] for t in range(ST)],
                                              g["ident"][:]))

                xt_fill(pe, g, ln, main, i)
                pe.wait_ge(ctx_in, (i + 1) * 16)
                for n, lhs, w, lo in (("k", ctx_t, wkv, 0), ("q", xt, wq, 0), ("v", ctx_t, wkv, D)):
                    for s in range(ST):
                        main.wait_for(pe, i, free=f"{n}{s}", drained=["xt2", "xt3"] if n == "q" else [])
                        main.fill(product(pe, bank(f"{n}{s}"), [(lhs[:, c, s * P:(s + 1) * P], w[:, c, lo:lo + D])
                                                                for c in range(CC if n != "q" else DC)]))
                for gr in range(NG):
                    for n, split, rope_done in (("k", k_split, k_rope), ("q", q_split, q_rope)):
                        if gr == 0:
                            pe.wait_ge(rope_done, (i + 1) * ST)
                        main.wait_for(pe, i, free=f"t{n}{gr}")
                        main.fill(transpose_group(pe, bank(f"t{n}{gr}"), [
                            split[:, s, gr * HG:(gr + 1) * HG, :].rearrange("p h r -> p (h r)") for s in range(ST)],
                            g["ident"][:]))
                for job in L1_ORDER:
                    {"m": max_job, "r": rows_job, "s": score_job, "v": value_jobs, "t": turn_out}[job[0]](*job[1:])
                for c in range(DC):
                    main.wait_for(pe, i, free=f"at{c}", drained=[f"ot{NG - 1}"])
                    main.fill(transpose_group(pe, bank(f"at{c}"), [attn[:, s, c * P:(c + 1) * P] for s in range(ST)],
                                              g["ident"][:]))
                for l in range(ST):
                    main.wait_for(pe, i, free=f"out{l}", drained=[f"at{DC - 1}"])
                    main.fill(product(pe, bank(f"out{l}"), [(g["ones"][0:1, :], bout[:])]
                                      + [(xt[:, c, l * P:(l + 1) * P], wout[:, c, :]) for c in range(DC)]))

        @blk.scalar
        def _(act):
            for ring in (main, score, outr):
                ring.credit(act, "act")
            act.wait_ge(ones_done, 3 * 2 * SETS + 1)
            with act.Fori(0, NB) as i:
                xt_drain(act, "act", g, main, i, xt)
                for n, raw, rope_done in (("k", k_raw, k_rope), ("q", q_raw, q_rope)):
                    for s in range(ST):
                        if s >= 2:
                            act.wait_ge(rope_done, i * ST + s - 1)
                        main.wait_filled(act, i, f"{n}{s}")
                        copy(act, "act", main, f"{n}{s}", raw[:, s % 2].rearrange("p a b -> p (a b)"), bank(f"{n}{s}"))
                for s in range(ST):
                    main.wait_filled(act, i, f"v{s}")
                    copy(act, "act", main, f"v{s}",
                         v[:, s, 0:H1 * VW].rearrange("p (h w) -> p h w", w=VW)[:, :, 0:HD],
                         bank(f"v{s}").rearrange("p (h w) -> p h w", w=HD))
                act.dma_start(ctx_t[:], ctx_src[:, :, bass.ts((i + 1) & 3, S)]).then_inc(ctx_in, 16)
                for gr in range(NG):
                    slot = (2 * gr) % SLOTS
                    act.wait_ge(staged_out[slot], (i * (2 * NG // SLOTS) + 2 * gr // SLOTS) * 16 + 1)
                    main.wait_filled(act, i, f"tk{gr}")
                    copy(act, "act", main, f"tk{gr}", slots[slot], bank(f"tk{gr}"))

                def out_copy(gr):
                    if gr > 0:
                        main.wait_filled(act, i, f"ot{gr - 1}")
                    outr.wait_filled(act, i, f"o{gr}")
                    copy(act, "act", outr, f"o{gr}", o_sb[:], bank(f"o{gr}", outr))

                for gr in range(NG):
                    for kt in range(ST):
                        if kt == 1 and gr > 0:
                            out_copy(gr - 1)
                        for j in (0, 2):
                            job = f"s{gr}_{kt}_{j}"
                            score.wait_filled(act, i, f"s{gr}_{kt}_{j + 1}")
                            b = score.bank(job)
                            score.drain(act.activation(probs[:, kt % 2, j:j + 2, :], g["psum"][:, b:b + 2, :], ACT.Exp,
                                                       scale=HD ** -0.5), job, banks=2)
                out_copy(NG - 1)
                for c in range(DC):
                    main.wait_filled(act, i, f"at{c}")
                    copy(act, "act", main, f"at{c}", xt[:, c, :], bank(f"at{c}"))

        @blk.vector
        def _(dve):
            for k in range(SETS):
                for m in (qs[k], ks[k]):
                    dve.memset(m[0:64].bitcast(F32), 0.0).then_inc(ones_done, 1)
                    dve.memset(m[64:128].bitcast(F32), 0.0).then_inc(ones_done, 1)
            dve.memset(v[:], 1.0).then_inc(ones_done, 1)
            dve.wait_ge(ones_done, 4 * SETS + 1)
            for k in range(SETS):
                dve.memset(ks[k][64:66].bitcast(F32), 1.0).then_inc(ones_done, 2)
            main.credit(dve, "dve")
            ln.credit(dve)
            st = Steps(q_steps, ST * ROPE_STEPS)
            with dve.Fori(0, NB) as i:
                st.begin(i)
                xt_drain(dve, "dve", g, main, i, xt)
                dve.wait_ge(main.drained_sem["dve"], (i + 1) * main.who.count("dve"))
                ln.vector(dve, i, (i + 1) & 3, lambda: main.wait_filled(dve, i, "xt3"))
                for s in range(ST):
                    main.wait_for(dve, i, drained=[f"q{s}"])
                    if s > 0:
                        dve.wait_ge(q_rope, i * ST + s)
                    rope_tile(dve, st, g, q_raw[:, s % 2], q_prod, q_rot, q_split[:, s],
                              i * ST + s).then_inc(q_rope, 1)
                for gr in range(NG):
                    slot = (2 * gr + 1) % SLOTS
                    dve.wait_ge(staged_out[slot], (i * (2 * NG // SLOTS) + 2 * gr // SLOTS) * 16 + 1)
                    main.wait_filled(dve, i, f"tq{gr}")
                    copy(dve, "dve", main, f"tq{gr}", slots[slot], bank(f"tq{gr}"))

                def maxima(h, t):
                    gr, j = divmod(h, HG)
                    job = f"m{h}_{t}"
                    main.wait_filled(dve, i, job)
                    main.drain(dve.tensor_reduce(mx[:, gr % 2, j, t:t + 1], bank(job), AX.X, ALU.max), job)
                    if (j, t) == (HG - 1, ST - 1):
                        n = HG * ST
                        m = mx[:, gr % 2].rearrange("p j t -> p (j t)")
                        main.wait_for(dve, i, drained=[job])
                        dve.tensor_scalar(mx_split[:, gr % 2, 0:n].bitcast(F32R), m, -1.0, None,
                                          ALU.mult).then_inc(mx_hi, 1)
                        dve.wait_ge(mx_hi, i * NG + gr + 1)
                        dve.scalar_tensor_tensor(mx_split[:, gr % 2, n:2 * n], m, -1.0, mx_split[:, gr % 2, 0:n],
                                                 ALU.mult, ALU.subtract).then_inc(mx_lo, 1)

                def rows_copy(gr):
                    if gr >= 2:
                        dve.wait_ge(row_out, (i * NG + gr - 1) * 16)
                    main.wait_filled(dve, i, f"nm{gr}")
                    copy(dve, "dve", main, f"nm{gr}", rows[:, gr % 2, :], bank(f"nm{gr}")[0:2 * HG * ST, 0:P])

                def divide(gr):
                    main.wait_filled(dve, i, f"ot{gr}")
                    b = bank(f"ot{gr}").rearrange("p (t j r) -> p t j r", t=ST, j=HG)
                    if gr > 0:
                        main.wait_for(dve, i, drained=[f"ot{gr - 1}"])
                    dve.reciprocal(inv[:, gr % 2], b[:, :, :, HD]).then_inc(inv_done, 1)
                    dve.wait_ge(inv_done, i * NG + gr + 1)
                    out = attn[:, :, gr * HG * HD:(gr + 1) * HG * HD].rearrange("p t (j r) -> p t j r", j=HG)
                    main.drain(dve.tensor_tensor(out, b[:, :, :, 0:HD],
                                                 inv[:, gr % 2].unsqueeze(3).to_broadcast([P, ST, HG, HD]), ALU.mult),
                               f"ot{gr}")

                for job in L1_ORDER:
                    if job[0] in "mrt":
                        {"m": maxima, "r": rows_copy, "t": divide}[job[0]](*job[1:])
                for l in range(ST):
                    residual(dve, main, i, f"out{l}", g, i * ST + l, g["gate"][:, 1:2])
                st.end()

        @blk.gpsimd
        def _(pool):
            st = Steps(k_steps, ST * ROPE_STEPS)
            with pool.Fori(0, NB) as i:
                st.begin(i)
                ln.pool(pool, i)
                for s in range(ST):
                    main.wait_for(pool, i, drained=[f"k{s}"])
                    if s > 0:
                        pool.wait_ge(k_rope, i * ST + s)
                    rope_tile(pool, st, g, k_raw[:, s % 2], k_prod, k_rot, k_split[:, s],
                              i * ST + s).then_inc(k_rope, 1)
                st.end()


def l1_order():
    order = [("m", h, t) for h in range(HG) for t in range(ST)] + [("r", 0)]
    order += [("m", HG + j, t) for j in range(HG // 2) for t in range(ST)]
    for gr in range(NG):
        for kt in range(ST):
            h = (gr + 1) * HG + 2 + kt
            ms = [("m", h, t) for t in range(ST)] if h < H1 else []
            order += [("s", gr, kt, 0), ("s", gr, kt, 1)] + ms[0:1] + [("s", gr, kt, 2), ("s", gr, kt, 3)] + ms[1:2]
            if (gr, kt) > (0, 0):
                order.append(("v", gr, kt - 1) if kt else ("v", gr - 1, ST - 1))
            order += ms[2:4]
            if kt == 2 and gr + 1 < NG:
                order.append(("r", gr + 1))
            if kt == 1 and gr > 0:
                order.append(("t", gr - 1))
    return order + [("v", NG - 1, ST - 1), ("t", NG - 1)]


L1_ORDER = l1_order()


def l1_main_order():
    jobs = []
    for job in L1_ORDER:
        if job[0] in "mrt":
            name = {"m": "m{}_{}", "r": "nm{}", "t": "ot{}"}[job[0]].format(*job[1:])
            jobs.append((name, "dve"))
    return jobs + [(f"at{c}", "act") for c in range(DC)] + [(f"out{l}", "dve") for l in range(ST)]


I1 = 2048
IC = I1 // P
QMAX, QMIN = 127.0, -128.0
BLK = 512
HA_STEPS = 12


def quantised(dve, st, out, in_, factor, hi, lo):
    st.inc(dve.tensor_scalar(out, in_, factor, hi, ALU.mult, ALU.min))
    st.wait(dve)
    st.inc(dve.tensor_scalar(out, out, lo, ROUND, ALU.max, ALU.add))


def l1_ffn(nc, g, a):
    with Phase(nc, "l1f") as ph:
        sem, sb = ph.sem, ph.sb
        w_in = sb("w_in", [P, 4 * I1])
        w_gate, w_up = [sb(n, [P, DC, I1], BF16) for n in ("w_gate", "w_up")]
        w_down = sb("w_down", [P, IC, D], BF16)
        had = sb("had", [P, P])
        w_sum, w_abs = sb("w_sum", [P, 3]), sb("w_abs", [P, 3, 3])
        tmp = sb("tmp", [P, ST, D])
        xq, xqt = sb("xq", [P, ST, D], BF16), sb("xqt", [P, DC, S], BF16)
        xs = sb("xs", [P, 6, ST])
        wide = sb("wide", [P, 4 * I1])
        raw = [w_in, wide, w_in]
        silu, mid, z0, z1 = [wide[:, k * I1:(k + 1) * I1] for k in range(4)]
        mid_t = sb("mid_t", [P, IC, P])
        half = sb("half", [P, I1 // 2])
        ys = sb("ys", [P, 4, 6])
        yq, yt = sb("yq", [P, 2, I1], BF16), sb("yt", [P, IC, P], BF16)

        slots = []
        for s in range(ST):
            slots.append({
                "it": [(f"it{s}_{n}", "dve" if n % 2 else "act") for n in range(4)],
                "gu": [(f"{k}{s}_{n}", w) for n in range(4) for k, w in (("g", "act"), ("u", "dve"))],
                "ha": [(f"ha{s}_{n}", "act" if n >= 2 else "dve") for n in (2, 3, 0, 1)],
                "dn": [(f"yt{s}_0", "act"), (f"yt{s}_1", "act"), (f"dn{s}", "dve")]})
        order = [("xq0", "act"), ("xq1", "act")] + [j for sl in slots for k in ("it", "gu", "ha", "dn") for j in sl[k]]
        order += [(f"spare{k}", None) for k in range(-len(order) % 8)]
        ring = Ring(sem, "l1f", range(8), order)
        names = [{k: [j for j, _ in v] for k, v in sl.items()} for sl in slots]
        (had_in, summed, tot_ready, tern_ready, w_steps, x_steps, z_steps, x_ready, xq_done,
         mid_ready, pool_steps, y_ready, yq_done, z_in) = [sem(n) for n in (
             "had_in", "summed", "tot_ready", "tern_ready", "w_steps", "x_steps", "z_steps",
             "x_ready", "xq_done", "mid_ready", "pool_steps", "y_ready", "yq_done", "z_in")]
        weight_in, scaled = [sem(f"weight_in{k}") for k in range(3)], sem("scaled")
        ln = LayerNorm(g, sem)
        blk = ph.block()
        weights = [("l1_gate", w_gate), ("l1_up", w_up), ("l1_down", w_down)]

        def bank(job):
            return g["psum"][:, ring.bank(job), :]

        def bank_bf(job):
            return bank(job).bitcast(BF16)

        def run(eng, f, start):
            def body(i, first, tail):
                start(i, tail)
                for s in range(ST):
                    turned = not (first and s < 1) and not (tail and s > 0)
                    f(i, s, "it", turned, tail)
                    f(i, s, "gu", not tail, tail)
                    f(i, s, "ha", turned, tail)
                    f(i, s, "dn", not (first and s < 2) and not (tail and s > 1), tail)
                    f(i, s, "end", turned, tail)
            body(0, True, False)
            with eng.Fori(1, NB) as i:
                body(i, False, False)
            body(NB, False, True)

        @blk.sync
        def _(sp):
            sp.dma_start(had[:], a["hadamard"]).then_inc(had_in, 16)
            for k, (name, w) in enumerate(weights):
                if k == 2:
                    sp.wait_ge(tern_ready, 1)
                c = w.shape[1]
                sp.dma_start(raw[k][:].rearrange("p (c n) -> p c n", c=c),
                             a[name].rearrange("(c p) n -> p c n", p=P)).then_inc(weight_in[k], 16)

        @blk.tensor
        def _(pe):
            for k in range(3):
                pe.wait_ge(summed, k + 1)
                pe.matmul(g["psum"][:, 7, k:k + 1], g["ones"][:], w_sum[:, k:k + 1], start=True,
                          stop=True).then_inc(tot_ready, 1)
            pe.wait_ge(tern_ready, 3)
            pe.wait_ge(had_in, 16)

            def start(i, tail):
                if tail:
                    ring.skip_fill(pe, i, ["xq0", "xq1"])
                    return
                pe.wait_ge(xq_done, i + 1)
                for k in range(2):
                    ring.wait_for(pe, i, free=f"xq{k}")
                    for c in (2 * k, 2 * k + 1):
                        for s in range(ST):
                            last = pe.transpose(bank_bf(f"xq{k}")[:, ((c % 2) * ST + s) * P:((c % 2) * ST + s + 1) * P],
                                                xq[:, s, c * P:(c + 1) * P], g["ident_bf"][:])
                    ring.fill(last)

            def stage(i, s, what, on, tail):
                if what == "end":
                    return
                if not on:
                    ring.skip_fill(pe, i, names[s][what])
                elif what == "it":
                    pe.wait_ge(mid_ready, i * ST + s)
                    for n in range(4):
                        ring.wait_for(pe, i, free=f"it{s}_{n}")
                        ring.fill(transpose_group(pe, bank(f"it{s}_{n}"), [mid[:, (4 * n + m) * P:(4 * n + m + 1) * P]
                                                                          for m in range(4)], g["ident"][:]))
                elif what == "gu":
                    for n in range(4):
                        for k, w in (("g", w_gate), ("u", w_up)):
                            ring.wait_for(pe, i, free=f"{k}{s}_{n}", drained=["xq1"])
                            ring.fill(product(pe, bank(f"{k}{s}_{n}"), [
                                (xqt[:, c, s * P:(s + 1) * P], w[:, c, n * BLK:(n + 1) * BLK]) for c in range(DC)]))
                elif what == "ha":
                    for n in (2, 3, 0, 1):
                        ring.wait_for(pe, i, free=f"ha{s}_{n}", drained=[f"it{s}_2", f"it{s}_3"])
                        for m in range(4):
                            last = pe.matmul(bank(f"ha{s}_{n}")[:, m * P:(m + 1) * P], mid_t[:, 4 * n + m, :], had[:],
                                             start=True, stop=True)
                        ring.fill(last)
                else:
                    pe.wait_ge(yq_done, i * ST + s - 1)
                    for k in range(2):
                        ring.wait_for(pe, i, free=f"yt{s}_{k}")
                        for m in range(8):
                            last = pe.transpose(bank_bf(f"yt{s}_{k}")[:, m * P:(m + 1) * P],
                                                yq[:, s % 2, (8 * k + m) * P:(8 * k + m + 1) * P], g["ident_bf"][:])
                        ring.fill(last)
                    ring.wait_for(pe, i, free=f"dn{s}", drained=[f"yt{s}_1"])
                    ring.fill(product(pe, bank(f"dn{s}"), [(yt[:, c, :], w_down[:, c, :]) for c in range(IC)]))
            run(pe, stage, start)

        @blk.scalar
        def _(act):
            ring.credit(act, "act")
            for k, (_, w) in enumerate(weights):
                act.wait_ge(w_steps, 5 * (k + 1))
                act.activation(w[:].rearrange("p c n -> p (c n)"), raw[k][:], ACT.Copy,
                               bias=-ROUND).then_inc(tern_ready, 1)

            def x_round():
                act.activation(xq[:].rearrange("p s d -> p (s d)"), tmp[:].rearrange("p s d -> p (s d)"), ACT.Copy,
                               bias=-ROUND).then_inc(xq_done, 1)
            act.wait_ge(x_ready, 1)
            x_round()

            def start(i, tail):
                if tail:
                    ring.skip_drain(act, i, "act", ["xq0", "xq1"])
                    return
                act.wait_ge(scaled, (i + 1) * 2)
                for k in range(2):
                    ring.wait_filled(act, i, f"xq{k}")
                    copy(act, "act", ring, f"xq{k}", xqt[:, 2 * k:2 * k + 2, :].rearrange("p c n -> p (c n)"),
                         bank_bf(f"xq{k}"))

            def stage(i, s, what, on, tail):
                if what == "end":
                    if on:
                        act.wait_ge(y_ready, i * ST + s)
                        act.activation(yq[:, (s + 1) % 2, :], z0[:], ACT.Copy, bias=-ROUND).then_inc(yq_done, 1)
                    if s == 1 and not tail:
                        act.wait_ge(x_ready, i + 2)
                        x_round()
                elif not on:
                    ring.skip_drain(act, i, "act", names[s][what])
                elif what == "it":
                    for n in (0, 2):
                        ring.wait_filled(act, i, f"it{s}_{n}")
                        copy(act, "act", ring, f"it{s}_{n}", mid_t[:, 4 * n:4 * n + 4, :].rearrange("p c n -> p (c n)"),
                             bank(f"it{s}_{n}"))
                elif what == "gu":
                    for n in range(4):
                        act.wait_ge(mid_ready, i * ST + s)
                        ring.wait_filled(act, i, f"g{s}_{n}")
                        ring.drain(act.activation(silu[:, n * BLK:(n + 1) * BLK], bank(f"g{s}_{n}"), ACT.Silu,
                                                  scale=xs[:, 4, s:s + 1]), f"g{s}_{n}")
                elif what == "ha":
                    act.wait_ge(z_in, i * ST + s - 1)
                    for n in (2, 3):
                        ring.wait_filled(act, i, f"ha{s}_{n}")
                        copy(act, "act", ring, f"ha{s}_{n}", half[:, (n - 2) * BLK:(n - 1) * BLK], bank(f"ha{s}_{n}"))
                else:
                    for k in range(2):
                        ring.wait_filled(act, i, f"yt{s}_{k}")
                        copy(act, "act", ring, f"yt{s}_{k}", yt[:, 8 * k:8 * k + 8, :].rearrange("p c n -> p (c n)"),
                             bank_bf(f"yt{s}_{k}"))
            run(act, stage, start)

        @blk.vector
        def _(dve):
            ws = Steps(w_steps, 15)
            ws.begin(0)
            for k in range(3):
                dve.wait_ge(weight_in[k], 16)
                dve.tensor_reduce(w_sum[:, k:k + 1], raw[k][:], AX.X, ALU.add,
                                  apply_absolute_value=True).then_inc(summed, 1)
                dve.wait_ge(tot_ready, k + 1)
                ws.inc(dve.tensor_scalar(w_abs[:, 0, k:k + 1], g["psum"][:, 7, k:k + 1], 1.0 / (D * I1), LN_EPS,
                                         ALU.mult, ALU.max))
                ws.wait(dve)
                ws.inc(dve.reciprocal(w_abs[:, 1, k:k + 1], w_abs[:, 0, k:k + 1]))
                ws.inc(dve.tensor_scalar(w_abs[:, 2, k:k + 1], w_abs[:, 0, k:k + 1],
                                         g["gate"][:, 5:6] if k == 2 else 1.0, None, ALU.mult))
                ws.wait(dve)
                quantised(dve, ws, raw[k][:], raw[k][:], w_abs[:, 1, k:k + 1], 1.0, -1.0)
            ws.end()
            ring.credit(dve, "dve")
            ln.credit(dve)
            xst = Steps(x_steps, 3 + 2 * ST - 1)
            zst = Steps(z_steps, ST * HA_STEPS)

            def scales():
                dve.tensor_scalar(xs[:, 4, :], xs[:, 1, :], w_abs[:, 0, 0:1], None, ALU.mult).then_inc(scaled, 1)
                dve.tensor_scalar(xs[:, 5, :], xs[:, 1, :], w_abs[:, 0, 1:2], None, ALU.mult).then_inc(scaled, 1)

            def quantise_x(i):
                xst.begin(i)
                xst.inc(dve.tensor_reduce(xs[:, 0, :], g["xn"][:], AX.X, ALU.max, apply_absolute_value=True))
                xst.wait(dve)
                xst.inc(dve.tensor_scalar(xs[:, 1, :], xs[:, 0, :], LN_EPS, 1.0 / -QMIN, ALU.max, ALU.mult))
                xst.wait(dve)
                xst.inc(dve.reciprocal(xs[:, 2, :], xs[:, 1, :]))
                xst.wait(dve)
                for s in range(ST):
                    xst.inc(dve.tensor_scalar(tmp[:, s, :], g["xn"][:, s, :], xs[:, 2, s:s + 1], QMAX, ALU.mult, ALU.min))
                xst.wait(dve)
                for s in range(ST - 1):
                    xst.inc(dve.tensor_scalar(tmp[:, s, :], tmp[:, s, :], QMIN, ROUND, ALU.max, ALU.add))
                xst.wait(dve)
                s = ST - 1
                dve.tensor_scalar(tmp[:, s, :], tmp[:, s, :], QMIN, ROUND, ALU.max, ALU.add).then_inc(x_ready, 1)
                xst.end()

            def start(i, tail):
                zst.begin(i)

            def stage(i, s, what, on, tail):
                if what == "end":
                    if s == ST - 1:
                        zst.end()
                    if s == 0 and not tail:
                        ring.wait_for(dve, i, drained=["dn0"])
                        ln.vector(dve, i, (i + 1) & 3, lambda: dve.wait_ge(xq_done, i + 1))
                    if s == 1 and not tail:
                        ln.wait_xn(dve, i + 1)
                        quantise_x(i + 1)
                    if s == ST - 1 and not tail:
                        scales()
                        dve.wait_ge(scaled, (i + 2) * 2)
                elif not on:
                    ring.skip_drain(dve, i, "dve", names[s][what])
                    if what == "ha":
                        if not (zst.n == 0 and s == 0 and not tail):
                            zst.wait(dve)
                        dve.sem_inc(z_steps, HA_STEPS)
                        zst.n += HA_STEPS
                elif what == "it":
                    for n in (1, 3):
                        ring.wait_filled(dve, i, f"it{s}_{n}")
                        copy(dve, "dve", ring, f"it{s}_{n}", mid_t[:, 4 * n:4 * n + 4, :].rearrange("p c n -> p (c n)"),
                             bank(f"it{s}_{n}"))
                elif what == "gu":
                    ring.wait_filled(dve, i, f"g{s}_0")
                    for n in range(4):
                        ring.wait_for(dve, i, drained=[f"g{s}_{n}"])
                        ring.wait_filled(dve, i, f"u{s}_{n}")
                        ins = dve.scalar_tensor_tensor(mid[:, n * BLK:(n + 1) * BLK], bank(f"u{s}_{n}"),
                                                       xs[:, 5, s:s + 1], silu[:, n * BLK:(n + 1) * BLK],
                                                       ALU.mult, ALU.mult)
                        ring.drain(ins, f"u{s}_{n}")
                    ring.wait_for(dve, i, drained=[f"u{s}_3"])
                    dve.sem_inc(mid_ready, 1)
                elif what == "ha":
                    ring.wait_for(dve, i, drained=[f"ha{s}_3"])
                    dve.wait_ge(yq_done, i * ST + s - 1)
                    for n in (0, 1):
                        ring.wait_filled(dve, i, f"ha{s}_{n}")
                        lo, hi = slice(n * BLK, (n + 1) * BLK), slice((n + 2) * BLK, (n + 3) * BLK)
                        zst.inc(dve.tensor_tensor(z0[:, lo], bank(f"ha{s}_{n}"), half[:, lo], ALU.add))
                        ring.drain(dve.tensor_tensor(z0[:, hi], bank(f"ha{s}_{n}"), half[:, lo], ALU.subtract),
                                   f"ha{s}_{n}")
                    zst.wait(dve)
                    ring.wait_for(dve, i, drained=[f"ha{s}_1"])
                    dve.sem_inc(z_in, 1)
                    dve.wait_ge(pool_steps, (i * ST + s) * 2)
                    for src, dst, h in ((z1, z0, 2), (z0, z1, 1)):
                        u, w = [m[:].rearrange("p (u two h) -> p u two h", two=2, h=h * P) for m in (src, dst)]
                        zst.inc(dve.tensor_tensor(w[:, :, 0, :], u[:, :, 0, :], u[:, :, 1, :], ALU.add))
                        zst.inc(dve.tensor_tensor(w[:, :, 1, :], u[:, :, 0, :], u[:, :, 1, :], ALU.subtract))
                        zst.wait(dve)
                    y, k = ys[:, s], 1.0 / np.sqrt(I1)
                    zst.inc(dve.tensor_reduce(y[:, 0:1], z1[:], AX.X, ALU.max, apply_absolute_value=True))
                    zst.wait(dve)
                    zst.inc(dve.tensor_scalar(y[:, 1:2], y[:, 0:1], float(k), LN_EPS, ALU.mult, ALU.max))
                    zst.wait(dve)
                    zst.inc(dve.reciprocal(y[:, 2:3], y[:, 1:2]))
                    zst.inc(dve.tensor_scalar(y[:, 4:5], y[:, 1:2], w_abs[:, 2, 2:3], 1.0 / -QMIN, ALU.mult, ALU.mult))
                    zst.wait(dve)
                    zst.inc(dve.tensor_scalar(y[:, 3:4], y[:, 2:3], float(k), -QMIN, ALU.mult, ALU.mult))
                    zst.wait(dve)
                    zst.inc(dve.tensor_scalar(z0[:], z1[:], y[:, 3:4], QMAX, ALU.mult, ALU.min))
                    zst.wait(dve)
                    dve.tensor_scalar(z0[:], z0[:], QMIN, ROUND, ALU.max, ALU.add).then_inc(y_ready, 1)
                else:
                    ring.wait_filled(dve, i, f"dn{s}")
                    tile = (i * ST + s - 2)
                    ring.drain(dve.scalar_tensor_tensor(g["x"][:, tile, :], bank(f"dn{s}"), ys[:, (s + 3) % 4, 4:5],
                                                        g["x"][:, tile, :], ALU.mult, ALU.add), f"dn{s}")
            quantise_x(0)
            scales()
            dve.wait_ge(scaled, 2)
            run(dve, stage, start)

        @blk.gpsimd
        def _(pool):
            def stage(i, s, what, on, tail):
                if what == "ha" and on:
                    pool.wait_ge(z_in, i * ST + s)
                    u, w = [m[:].rearrange("p (u two h) -> p u two h", two=2, h=4 * P) for m in (z0, z1)]
                    pool.tensor_tensor(w[:, :, 0, :], u[:, :, 0, :], u[:, :, 1, :], ALU.add).then_inc(pool_steps, 1)
                    pool.tensor_tensor(w[:, :, 1, :], u[:, :, 0, :], u[:, :, 1, :], ALU.subtract).then_inc(pool_steps, 1)
                if what == "end" and s == 0 and not tail:
                    ln.pool(pool, i)
            run(pool, stage, lambda i, tail: None)


def load_xt_all(ph, g, ln, xt_all, xt_lo=None):
    ring = Ring(ph.sem, ph.tag + "_xt", range(4), xt_jobs() if xt_lo is None else [(f"xt{c}", "dve") for c in range(DC)])
    hi_done = ph.sem("xt_hi_done")

    def tensor(pe):
        with pe.Fori(0, NB) as i:
            xt_fill(pe, g, ln, ring, i)
        ring.wait_for(pe, NB - 1, drained=["xt2", "xt3"])

    def scalar(act):
        if xt_lo is None:
            ring.credit(act, "act")
        with act.Fori(0, NB) as i:
            if xt_lo is None:
                xt_drain(act, "act", g, ring, i, xt_all[:, :, bass.ts(i, S)])
            else:
                for c in range(DC):
                    ring.wait_filled(act, i, f"xt{c}")
                    act.activation(xt_all[:, c, bass.ts(i, S)], g["psum"][:, ring.bank(f"xt{c}"), :],
                                   ACT.Copy).then_inc(hi_done, 1)

    def vector(dve):
        ring.credit(dve, "dve")
        ln.credit(dve)
        with dve.Fori(0, NB) as i:
            ln.vector(dve, i, (i + 1) & 3, lambda: ring.wait_filled(dve, i, "xt3"))
            if xt_lo is None:
                xt_drain(dve, "dve", g, ring, i, xt_all[:, :, bass.ts(i, S)])
            else:
                for c in range(DC):
                    dve.wait_ge(hi_done, i * DC + c + 1)
                    ring.drain(dve.tensor_tensor(xt_lo[:, c, bass.ts(i, S)], g["psum"][:, ring.bank(f"xt{c}"), :],
                                                 xt_all[:, c, bass.ts(i, S)].bitcast(F32), ALU.subtract), f"xt{c}")

    def pool(pool):
        with pool.Fori(0, NB) as i:
            ln.pool(pool, i)
    return tensor, scalar, vector, pool


H2 = 16
G2 = H2 // 4
V_FIRST, V_LATER = (0, 1), (2, 3)


def l2_xattn(nc, g, a):
    with Phase(nc, "l2x") as ph:
        sem, sb = ph.sem, ph.sb
        xt_all = sb("xt_all", [P, DC, NB * S])
        wq, wk, wv, wo = [[sb(f"{n}{k}", [P, c, D]) for k in range(2)]
                          for n, c in (("wq", DC), ("wk", CC), ("wv", CC), ("wo", 4))]
        gains = sb("gains", [P, 3])
        ctx_t = sb("ctx_t", [P, CC, S])
        k_tok, v_tok = sb("k_tok", [P, ST, D]), sb("v_tok", [P, ST, D])
        sq = sb("sq", [P, 4, S])
        qt, kt = sb("qt", [P, 4, S]), sb("kt", [P, 4, S])
        norms = sb("norms", [P, 4, 4, ST])
        probs, probs_t = sb("probs", [P, 3, ST, S]), sb("probs_t", [P, ST, S])
        soft = sb("soft", [P, 3, 4, ST])
        ot = sb("ot", [P, 4, S])
        order = ([(f"k{t}", "act") for t in range(ST)] + [(f"v{t}", "dve") for t in V_FIRST]
                 + [(f"q{h}", "act") for h in range(4)] + [("ssq", "dve")] + [(f"kt{h}", "dve") for h in range(4)])
        heads = l2_head_order()
        for what, h in heads:
            if what == "s":
                order += [(f"s{h}_{t}", "act") for t in range(ST)]
                if h == 0:
                    order += [(f"v{t}", "dve") for t in V_LATER]
            elif what == "t":
                order += [(f"pt{h}_{n}", "dve" if n % 2 else "act") for n in range(ST)]
            else:
                order += [(f"pv{h}", "act")]
        order += [(f"out{t}", "dve") for t in range(ST)]
        order += [(f"spare{k}", None) for k in range(-len(order) % 8)]
        ring = Ring(sem, "l2x", range(8), order)
        (gains_in, ctx_in, k_sq, k_sum, k_norm, q_ms, q_norm, gain_done, k_ready, max_ready, bias_ready, inv_ready,
         probs_ready) = [sem(n) for n in (
             "gains_in", "ctx_in", "k_sq", "k_sum", "k_norm", "q_ms", "q_norm", "gain_done", "k_ready", "max_ready",
             "bias_ready", "inv_ready", "probs_ready")]
        w_in = [sem(f"w_in{k}") for k in range(2)]
        k_ready_steps, pool_steps = sem("k_ready_steps"), sem("pool_steps")
        ln = LayerNorm(g, sem)
        xt_pe, xt_act, xt_dve, xt_pool = load_xt_all(ph, g, ln, xt_all)
        next_ln = LayerNorm(g, lambda n: sem(n + "_next"))
        blk = ph.block()
        ctx_src = a["ctx_t"].rearrange("(c p) n -> p c n", p=P)

        def bank(job):
            return g["psum"][:, ring.bank(job), :]

        def bodies(eng, body):
            with eng.Fori(0, G2 // 2) as pair:
                for k in range(2):
                    with eng.Fori(0, NB) as b:
                        body((pair * 2 + k) * NB + b, b, k, pair)

        @blk.sync
        def _(sp):
            for k, n in enumerate(("l2_gq", "l2_gk")):
                sp.dma_start(gains[:, k:k + 1], a[n].rearrange("(p o) -> p o", o=1)).then_inc(gains_in, 16)
            sp.dma_start(ctx_t[:], ctx_src[:, :, 0:S]).then_inc(ctx_in, 16)
            for gr in range(G2):
                if gr >= 2:
                    ring.wait_filled(sp, (gr - 2) * NB + NB - 1, f"out{ST - 1}")
                k, cols = gr % 2, slice(gr * D, (gr + 1) * D)
                for w, src in ((wk, a["l2_wk"][:, cols]), (wv, a["l2_wv"][:, cols]), (wq, a["l2_wq"][:, cols]),
                               (wo, a["l2_wo"][cols, :])):
                    sp.dma_start(w[k][:], src.rearrange("(c p) n -> p c n", p=P)).then_inc(w_in[k], 16)
            sp.wait_ge(ctx_in, (G2 * NB + 1) * 16)

        @blk.tensor
        def _(pe):
            xt_pe(pe)

            def body(i, b, k, pair):
                pe.wait_ge(w_in[k], (pair + 1) * 64)
                pe.wait_ge(ctx_in, (i + 1) * 16)

                def from_context(n, w, tiles):
                    for t in tiles:
                        ring.wait_for(pe, i, free=f"{n}{t}")
                        ring.fill(product(pe, bank(f"{n}{t}"), [(ctx_t[:, c, t * P:(t + 1) * P], w[k][:, c, :])
                                                                for c in range(CC)]))

                from_context("k", wk, range(ST))
                from_context("v", wv, V_FIRST)
                for h in range(4):
                    ring.wait_for(pe, i, free=f"q{h}")
                    ring.fill(product(pe, bank(f"q{h}"), [(wq[k][:, c, h * P:(h + 1) * P], xt_all[:, c, bass.ts(b, S)])
                                                          for c in range(DC)]))
                ring.wait_for(pe, i, free="ssq", drained=["q3"])
                for h in range(4):
                    for t in range(ST):
                        last = pe.matmul(bank("ssq")[:, h * ST + t:h * ST + t + 1], sq[:, h, t * P:(t + 1) * P],
                                         g["ones"][:, 0:1], start=True, stop=True)
                ring.fill(last)
                pe.wait_ge(k_ready, i + 1)
                for h in range(4):
                    ring.wait_for(pe, i, free=f"kt{h}")
                    ring.fill(transpose_group(pe, bank(f"kt{h}"), [k_tok[:, t, h * P:(h + 1) * P] for t in range(ST)],
                                              g["ident"][:]))
                for what, h in heads:
                    if what == "s":
                        for t in range(ST):
                            ring.wait_for(pe, i, free=f"s{h}_{t}", drained=[f"kt{h}"])
                            ring.fill(product(pe, bank(f"s{h}_{t}"), [(qt[:, h, t * P:(t + 1) * P], kt[:, h, :])]))
                        if h == 0:
                            from_context("v", wv, V_LATER)
                    elif what == "t":
                        pe.wait_ge(probs_ready, i * 4 * ST + (h + 1) * ST)
                        for n in range(ST):
                            ring.wait_for(pe, i, free=f"pt{h}_{n}")
                            ring.fill(transpose_group(pe, bank(f"pt{h}_{n}"), [
                                probs[:, h % 3, t, n * P:(n + 1) * P] for t in range(ST)], g["ident"][:]))
                    else:
                        ring.wait_for(pe, i, free=f"pv{h}", drained=[f"pt{h}_2", f"pt{h}_3"])
                        ring.fill(product(pe, bank(f"pv{h}"), [(v_tok[:, n, h * P:(h + 1) * P], probs_t[:, n, :])
                                                               for n in range(ST)]))
                for t in range(ST):
                    ring.wait_for(pe, i, free=f"out{t}", drained=["pv3"])
                    ring.fill(product(pe, bank(f"out{t}"), [(ot[:, h, t * P:(t + 1) * P], wo[k][:, h, :])
                                                            for h in range(4)]))
            bodies(pe, body)

        @blk.scalar
        def _(act):
            xt_act(act)
            ring.credit(act, "act")

            def body(i, b, k, pair):
                for t in range(ST):
                    ring.wait_filled(act, i, f"k{t}")
                    copy(act, "act", ring, f"k{t}", k_tok[:, t, :], bank(f"k{t}"))
                act.wait_ge(k_sum, i + 1)
                for h in range(4):
                    ring.wait_filled(act, i, f"q{h}")
                    act.activation(sq[:, h, :], bank(f"q{h}"), ACT.Square).then_inc(q_ms, 1)
                    act.wait_ge(q_ms, i * 4 + h + 1)
                    copy(act, "act", ring, f"q{h}", qt[:, h, :], bank(f"q{h}"))
                act.wait_ge(q_norm, i + 1)
                for what, h in heads:
                    if what == "s":
                        act.wait_ge(bias_ready, i * 4 + h + 1)
                        for t in range(ST):
                            ring.drain(act.activation(probs[:, h % 3, t, :], bank(f"s{h}_{t}"), ACT.Exp,
                                                      bias=soft[:, h % 3, 1, t:t + 1], scale=norms[:, 1, h, t:t + 1],
                                                      accum_out=soft[:, h % 3, 2, t:t + 1]), f"s{h}_{t}")
                        if h == 1:
                            ring.wait_filled(act, i, f"v{V_LATER[-1]}")
                            act.dma_start(ctx_t[:], ctx_src[:, :, bass.ts((b + 1) & 3, S)]).then_inc(ctx_in, 16)
                    elif what == "t":
                        for n in (0, 2):
                            ring.wait_filled(act, i, f"pt{h}_{n}")
                            copy(act, "act", ring, f"pt{h}_{n}", probs_t[:, n, :], bank(f"pt{h}_{n}"))
                    else:
                        ring.wait_filled(act, i, f"pv{h}")
                        copy(act, "act", ring, f"pv{h}", ot[:, h, :], bank(f"pv{h}"))
            bodies(act, body)

        @blk.vector
        def _(dve):
            xt_dve(dve)
            dve.wait_ge(gains_in, 32)
            dve.tensor_scalar(gains[:, 2:3], gains[:, 0:1], gains[:, 1:2], float(P ** -0.5), ALU.mult,
                              ALU.mult).then_inc(gain_done, 1)
            dve.wait_ge(gain_done, 1)
            ring.credit(dve, "dve")

            def body(i, b, k, pair):
                def copy_values(tiles):
                    for t in tiles:
                        ring.wait_filled(dve, i, f"v{t}")
                        copy(dve, "dve", ring, f"v{t}", v_tok[:, t, :], bank(f"v{t}"))

                dve.wait_ge(k_sq, i + 1)
                dve.tensor_reduce(norms[:, 2].rearrange("p h t -> p t h"),
                                  sq[:].rearrange("p t (h d) -> p t h d", h=4), AX.X, ALU.add).then_inc(k_sum, 1)
                copy_values(V_FIRST)
                dve.wait_ge(k_norm, i + 1)
                for t in range(ST):
                    view = k_tok[:, t, :].rearrange("p (h d) -> p h d", h=4)
                    ins = dve.tensor_tensor(view, view, norms[:, 3, :, t:t + 1].to_broadcast([P, 4, P]), ALU.mult)
                    ins.then_inc(k_ready_steps, 1)
                dve.wait_ge(k_ready_steps, (i + 1) * ST)
                dve.sem_inc(k_ready, 1)
                ring.wait_filled(dve, i, "ssq")
                ring.drain(dve.tensor_scalar(norms[:, 0].rearrange("p h t -> p (h t)"), bank("ssq")[:, 0:4 * ST],
                                             1.0 / P, LN_EPS, ALU.mult, ALU.add), "ssq")
                for h in range(4):
                    ring.wait_filled(dve, i, f"kt{h}")
                    ring.drain(dve.tensor_scalar(kt[:, h, :], bank(f"kt{h}"), gains[:, 2:3], None, ALU.mult), f"kt{h}")
                for what, h in l2_vector_order():
                    if what == "s":
                        for t in range(ST):
                            ring.wait_filled(dve, i, f"s{h}_{t}")
                            dve.tensor_reduce(soft[:, h % 3, 0, t:t + 1], bank(f"s{h}_{t}"), AX.X, ALU.max,
                                              negate=True).then_inc(max_ready, 1)
                        dve.wait_ge(max_ready, (i * 4 + h + 1) * ST)
                        dve.wait_ge(q_norm, i + 1)
                        dve.tensor_tensor(soft[:, h % 3, 1, :], soft[:, h % 3, 0, :], norms[:, 1, h, :],
                                          ALU.mult).then_inc(bias_ready, 1)
                        if h == 0:
                            copy_values(V_LATER)
                    elif what == "n":
                        ring.wait_for(dve, i, drained=[f"s{h}_{ST - 1}"])
                        dve.reciprocal(soft[:, h % 3, 3, :], soft[:, h % 3, 2, :]).then_inc(inv_ready, 1)
                        dve.wait_ge(inv_ready, i * 4 + h + 1)
                        for t in range(ST):
                            dve.tensor_scalar(probs[:, h % 3, t, :], probs[:, h % 3, t, :],
                                              soft[:, h % 3, 3, t:t + 1], None, ALU.mult).then_inc(probs_ready, 1)
                    else:
                        for n in (1, 3):
                            ring.wait_filled(dve, i, f"pt{h}_{n}")
                            copy(dve, "dve", ring, f"pt{h}_{n}", probs_t[:, n, :], bank(f"pt{h}_{n}"))
                for t in range(ST):
                    residual(dve, ring, i, f"out{t}", g, b * ST + t, g["gate"][:, 2:3])
            bodies(dve, body)
            ring.wait_for(dve, G2 * NB - 1, drained=[f"out{ST - 1}"])
            next_ln.vector(dve, 0, 0, lambda: None)

        @blk.gpsimd
        def _(pool):
            xt_pool(pool)

            def body(i, b, k, pair):
                ring.wait_for(pool, i, drained=[f"k{ST - 1}"])
                pool.tensor_tensor(sq[:], k_tok[:], k_tok[:], ALU.mult).then_inc(k_sq, 1)
                pool.wait_ge(k_sum, i + 1)
                pool.tensor_tensor(norms[:, 3], norms[:, 2], g["inv_p"][:].rearrange("p (h t) -> p h t", h=4), ALU.mult
                                   ).then_inc(pool_steps, 1)
                pool.wait_ge(pool_steps, i * 2 + 1)
                pool.tensor_tensor(norms[:, 3], norms[:, 3], g["eps"][:].rearrange("p (h t) -> p h t", h=4), ALU.add
                                   ).then_inc(pool_steps, 1)
                pool.wait_ge(pool_steps, i * 2 + 2)
                half = g["minus_half"][:].rearrange("p (h t) -> p h t", h=4)
                pool.tensor_tensor(norms[:, 3], norms[:, 3], half, ALU.pow).then_inc(k_norm, 1)
                ring.wait_for(pool, i, drained=["ssq"])
                pool.tensor_tensor(norms[:, 1], norms[:, 0], half, ALU.pow).then_inc(q_norm, 1)
            bodies(pool, body)
            next_ln.pool(pool, 0)


def l2_head_order():
    return [("s", 0), ("s", 1), ("t", 0), ("s", 2), ("v", 0), ("t", 1), ("s", 3), ("v", 1), ("t", 2), ("v", 2),
            ("t", 3), ("v", 3)]


def l2_vector_order():
    return [("s", 0), ("n", 0), ("s", 1), ("t", 0), ("n", 1), ("s", 2), ("t", 1), ("n", 2), ("s", 3), ("t", 2),
            ("n", 3), ("t", 3)]


E2, I2 = 8, 256
SHARED = 4
EALL = E2 + SHARED
NT = NB * ST


def l2_ffn(nc, g, a):
    with Phase(nc, "l2f") as ph:
        sem, sb = ph.sem, ph.sb
        xt_hi, xt_lo = [sb(n, [P, DC, NB * S], F32R) for n in ("xt_hi", "xt_lo")]
        router = sb("router", [P, DC, E2 + 1])
        raw = sb("raw", [P, 3 * DC * I2])
        w_split = [[sb(f"w_{n}{k}", [P, 3 * DC * I2], F32R) for n in ("hi", "lo")] for k in range(2)]
        w_gate, w_up, w_down = [[[part[:, m * DC * I2:(m + 1) * DC * I2].rearrange("p (c n) -> p c n", c=c)
                                  for part in w_split[k]] for k in range(2)] for m, c in ((0, DC), (1, DC), (2, 2))]
        prob = sb("prob", [P, NT, E2])
        col = sb("col", [P, 6, NT])
        top, top_at = sb("top", [P, NT, 8]), sb("top_at", [P, NT, 8], mybir.dt.uint32)
        top_f, lane = sb("top_f", [P, NT, 8]), sb("lane", [P, E2])
        first, second = sb("first", [P, NT, E2]), sb("second", [P, NT, E2])
        weight = sb("weight", [P, NT, EALL])
        silu, hidden = sb("silu", [P, 2, S]), sb("hidden", [P, 2, 2, S])
        hidden_hi, hidden_lo = [sb(n, [P, 2, 2, S], F32R) for n in ("hidden_hi", "hidden_lo")]
        slots = [(k, b) for k in range(2) for b in range(NB)]
        order = []
        for n, _ in enumerate(slots):
            order += [(f"g{n}_0", "act"), (f"u{n}_0", "dve"), (f"g{n}_1", "act"), (f"u{n}_1", "dve")]
            order += [(f"dn{n}_{t}", "dve") for t in range(ST)]
        ring = Ring(sem, "l2f", range(8), order)
        (router_in, route_filled, steps_sem, exp_ready, lane_ready, max_at, sig_ready, routed, hid_ready,
         tri) = [sem(n) for n in ("router_in", "route_filled", "steps", "exp_ready", "lane_ready", "max_at",
                                  "sig_ready", "routed", "hid_ready", "tri")]
        lane_steps = sem("lane_steps")
        raw_in, w_hi_done, w_lo_done, hid_hi_done = [sem(n) for n in (
            "raw_in", "w_hi_done", "w_lo_done", "hid_hi_done")]
        ln = LayerNorm(g, sem)
        xt_pe, xt_act, xt_dve, xt_pool = load_xt_all(ph, g, ln, xt_hi, xt_lo)
        next_ln = LayerNorm(g, lambda n: sem(n + "_next"))
        blk = ph.block()
        pairs = EALL // 2

        def split_next(eng, who, i, k):
            hi, lo = w_split[1 - k]
            if who == "act":
                eng.wait_ge(raw_in, (i * 2 + k + 2) * 48)
                ring.wait_filled(eng, i, f"dn{NB * k}_{ST - 1}")
                eng.activation(hi[:], raw[:], ACT.Copy).then_inc(w_hi_done, 1)
            else:
                eng.wait_ge(w_hi_done, i * 2 + k + 2)
                eng.tensor_tensor(lo[:], raw[:], hi[:].bitcast(F32), ALU.subtract).then_inc(w_lo_done, 1)

        def bank(job):
            return g["psum"][:, ring.bank(job), :]

        def run(eng, f):
            def body(i, head, tail):
                for n, (k, b) in enumerate(slots):
                    f(i, n, k, b, "gu", not tail)
                    f(i, n, k, b, "dn", not (head and n == 0) and not (tail and n > 0))
            body(0, True, False)
            with eng.Fori(1, pairs) as i:
                body(i, False, False)
            body(pairs, False, True)

        def names(n, what):
            return [f"{x}{n}_{m}" for m in range(2) for x in "gu"] if what == "gu" else [f"dn{n}_{t}" for t in range(ST)]

        @blk.sync
        def _(sp):
            sp.dma_start(router[:], a["l2_router"].rearrange("(c p) n -> p c n", p=P)).then_inc(router_in, 16)
            for e in range(EALL + 1):
                if e >= 1:
                    sp.wait_ge(w_lo_done, e)
                for m, n in enumerate(("l2_ge", "l2_ue", "l2_de")):
                    src = a[n][e % EALL].rearrange("(c p) n -> p c n", p=P)
                    sp.dma_start(raw[:, m * DC * I2:(m + 1) * DC * I2].rearrange("p (c n) -> p c n", c=src.shape[1]),
                                 src).then_inc(raw_in, 16)

        @blk.tensor
        def _(pe):
            xt_pe(pe)
            pe.wait_ge(router_in, 16)
            for t in range(NT):
                last = product(pe, g["psum"][:, 4, t * (E2 + 1):(t + 1) * (E2 + 1)],
                               [(part[:, c, t * P:(t + 1) * P].bitcast(F32), router[:, c, :])
                                for c in range(DC) for part in (xt_hi, xt_lo)])
            last.then_inc(route_filled, 1)

            def stage(i, n, k, b, what, on):
                if not on:
                    ring.skip_fill(pe, i, names(n, what))
                elif what == "gu":
                    if b == 0:
                        pe.wait_ge(w_lo_done, i * 2 + k + 1)
                    for m in range(2):
                        for x, w in (("g", w_gate), ("u", w_up)):
                            job = f"{x}{n}_{m}"
                            ring.wait_for(pe, i, free=job)
                            ring.fill(split_product(pe, bank(job), [
                                ([part[:, c, m * P:(m + 1) * P] for part in w[k]],
                                 [part[:, c, b * S:(b + 1) * S] for part in (xt_hi, xt_lo)]) for c in range(DC)]))
                else:
                    pn = (n - 1) % len(slots)
                    if isinstance(i, int) and i == 0 and n == 1:
                        pe.wait_ge(routed, 1)
                    pe.wait_ge(hid_ready, i * len(slots) * 2 + 2 * n)
                    for t in range(ST):
                        ring.wait_for(pe, i, free=f"dn{n}_{t}")
                        ring.fill(split_product(pe, bank(f"dn{n}_{t}"), [
                            ([part[:, pn % 2, m, t * P:(t + 1) * P] for part in (hidden_hi, hidden_lo)],
                             [part[:, m, :] for part in w_down[slots[pn][0]]]) for m in range(2)]))
            run(pe, stage)

        @blk.scalar
        def _(act):
            xt_act(act)
            act.wait_ge(raw_in, 48)
            act.activation(w_split[0][0][:], raw[:], ACT.Copy).then_inc(w_hi_done, 1)
            ring.credit(act, "act")
            act.wait_ge(tri, 1)
            act.activation(prob[:], prob[:], ACT.Exp).then_inc(exp_ready, 1)
            act.activation(col[:, 3, :], g["psum"][:, 4, 0:NT * (E2 + 1)].rearrange("p (t e) -> p t e", e=E2 + 1)[:, :, E2],
                           ACT.Exp, scale=-1.0).then_inc(sig_ready, 1)

            def stage(i, n, k, b, what, on):
                if not on:
                    ring.skip_drain(act, i, "act", names(n, what))
                elif what == "gu":
                    for m in range(2):
                        ring.wait_filled(act, i, f"g{n}_{m}")
                        ring.drain(act.activation(silu[:, m, :], bank(f"g{n}_{m}"), ACT.Silu), f"g{n}_{m}")
                    for m in range(2):
                        ring.wait_for(act, i, drained=[f"u{n}_{m}"])
                        act.activation(hidden_hi[:, n % 2, m, :], hidden[:, n % 2, m, :], ACT.Copy).then_inc(hid_hi_done, 1)
                    if b == 1:
                        split_next(act, "act", i, k)
            run(act, stage)

        @blk.vector
        def _(dve):
            xt_dve(dve)
            ring.credit(dve, "dve")
            st = Steps(steps_sem, 8 + 3 * NT + 5)
            st.begin(0)
            logits = g["psum"][:, 4, 0:NT * (E2 + 1)].rearrange("p (t e) -> p t e", e=E2 + 1)

            def wide(k):
                return col[:, k, :].unsqueeze(2).to_broadcast([P, NT, E2])

            dve.wait_ge(route_filled, 1)
            st.inc(dve.tensor_reduce(col[:, 0, :], logits[:, :, 0:E2], AX.X, ALU.max))
            st.wait(dve)
            dve.tensor_tensor(prob[:], logits[:, :, 0:E2], wide(0), ALU.subtract).then_inc(tri, 1)
            dve.wait_ge(exp_ready, 1)
            st.inc(dve.tensor_reduce(col[:, 1, :], prob[:], AX.X, ALU.add))
            st.wait(dve)
            st.inc(dve.reciprocal(col[:, 2, :], col[:, 1, :]))
            st.wait(dve)
            st.inc(dve.tensor_tensor(prob[:], prob[:], wide(2), ALU.mult))
            st.wait(dve)
            for t in range(NT):
                st.inc(dve.max(top[:, t, :], prob[:, t, :]))
            st.wait(dve)
            for t in range(NT):
                dve.max_index(top_at[:, t, :], top[:, t, :], prob[:, t, :]).then_inc(max_at, 1)
            st.inc(dve.tensor_tensor(col[:, 0, :], top[:, :, 0], top[:, :, 1], ALU.add))
            dve.wait_ge(max_at, NT)
            st.inc(dve.tensor_copy(top_f[:], top_at[:]))
            st.wait(dve)
            st.inc(dve.reciprocal(col[:, 1, :], col[:, 0, :]))
            st.wait(dve)
            st.inc(dve.tensor_scalar(col[:, 1, :], col[:, 1, :], g["gate"][:, 6:7], None, ALU.mult))
            st.wait(dve)
            dve.wait_ge(sig_ready, 1)
            st.inc(dve.tensor_scalar(col[:, 4, :], col[:, 3, :], 1.0, None, ALU.add))
            st.wait(dve)
            st.inc(dve.reciprocal(col[:, 5, :], col[:, 4, :]))
            st.wait(dve)
            dve.wait_ge(lane_ready, 1)
            for t in range(NT):
                for k, dst in ((0, first), (1, second)):
                    st.inc(dve.tensor_scalar(dst[:, t, :], lane[:], top_f[:, t, k:k + 1], top[:, t, k:k + 1],
                                             ALU.is_equal, ALU.mult))
            st.wait(dve)
            st.inc(dve.tensor_tensor(first[:], first[:], second[:], ALU.add))
            st.inc(dve.tensor_scalar(weight[:, :, E2:EALL], col[:, 5, :].unsqueeze(2).to_broadcast([P, NT, SHARED]),
                                     g["gate"][:, 6:7], None, ALU.mult))
            st.wait(dve)
            st.inc(dve.tensor_tensor(weight[:, :, 0:E2], first[:], wide(1), ALU.mult))
            st.wait(dve)
            dve.sem_inc(routed, 1)
            st.end()

            def stage(i, n, k, b, what, on):
                if not on:
                    ring.skip_drain(dve, i, "dve", names(n, what))
                elif what == "gu":
                    for m in range(2):
                        ring.wait_for(dve, i, drained=[f"g{n}_{m}"])
                        ring.wait_filled(dve, i, f"u{n}_{m}")
                        ring.drain(dve.tensor_tensor(hidden[:, n % 2, m, :], bank(f"u{n}_{m}"), silu[:, m, :],
                                                     ALU.mult), f"u{n}_{m}")
                else:
                    pn = (n - 1) % len(slots)
                    pk, pb = slots[pn]
                    e = i * 2 + pk - (2 if n == 0 else 0)
                    for t in range(ST):
                        tile = pb * ST + t
                        residual(dve, ring, i, f"dn{n}_{t}", g, tile, weight[:, tile, bass.ds(e, 1)])
            run(dve, stage)
            ring.wait_for(dve, pairs, drained=[f"dn0_{ST - 1}"])
            next_ln.vector(dve, 0, 0, lambda: None)

        @blk.gpsimd
        def _(pool):
            for e in range(E2):
                pool.memset(lane[:, e:e + 1], float(e)).then_inc(lane_steps, 1)
            pool.wait_ge(lane_steps, E2)
            pool.sem_inc(lane_ready, 1)
            xt_pool(pool)
            pool.wait_ge(w_hi_done, 1)
            pool.tensor_tensor(w_split[0][1][:], raw[:], w_split[0][0][:].bitcast(F32), ALU.subtract).then_inc(w_lo_done, 1)

            def stage(i, n, k, b, what, on):
                if on and what == "gu":
                    for m in range(2):
                        pool.wait_ge(hid_hi_done, i * len(slots) * 2 + 2 * n + m + 1)
                        pool.tensor_tensor(hidden_lo[:, n % 2, m, :], hidden[:, n % 2, m, :],
                                           hidden_hi[:, n % 2, m, :].bitcast(F32), ALU.subtract).then_inc(hid_ready, 1)
                    if b == 1:
                        split_next(pool, "pool", i, k)
            run(pool, stage)
            next_ln.pool(pool, 0)


NS = 16
RANK = 16
TAPS = 4
XD = RANK + 2 * NS
ATANH = (0.281746572692005, 0.27961418833618995, 0.40024853723539416, 0.6666631593507957, 2.0000000078777487)


def l3_xattn(nc, g, a):
    with Phase(nc, "l3x") as ph:
        u, dt = ph.sb("u", [P, DC, NB * S]), ph.sb("dt", [P, DC, NB * S])
        zs = ph.sb("zs", [P, ST, NB * S])
        a_neg, skip = ph.sb("a_neg", [P, DC, NS]), ph.sb("skip", [P, DC])
        xd_dram = nc.dram_tensor("l3x_xd_dram", [NB, 2, NS, S], F32).ap()
        l3_project(nc, g, a, u, dt, zs, a_neg, skip, xd_dram)
        l3_scan(nc, g, u, dt, zs, a_neg, skip, xd_dram)


def l3_project(nc, g, a, u, dt, zs, a_neg, skip, xd_dram):
    with Phase(nc, "l3p") as ph:
        sem, sb = ph.sem, ph.sb
        w_in_proj = sb("w_in_proj", [P, CC, D])
        w_x, w_dt = sb("w_x", [P, DC, XD]), sb("w_dt", [RANK, D])
        conv_w, conv_b = sb("conv_w", [P, DC, TAPS]), sb("conv_b", [P, DC])
        dt_b, two = sb("dt_b", [P, DC]), sb("two", [P, 1])
        ctx_t = sb("ctx_t", [P, CC, NB * S])
        padded = sb("padded", [P, 2, S + TAPS - 1])
        conv = sb("conv", [P, 2, S])
        xd = sb("xd", [XD, S])
        soft = sb("soft", [P, DC, 4, S])
        (weights_in, pad_ready, conv_steps, conv_done, u_ready, a_exp, xd_ready, xd_out, soft_act, dt_ready,
         z_ready) = [sem(n) for n in ("weights_in", "pad_ready", "conv_steps", "conv_done", "u_ready", "a_exp",
                                      "xd_ready", "xd_out", "soft_act", "dt_ready", "z_ready")]
        a_done, s_ready, q_ready, horner = [sem(n) for n in ("a_done", "s_ready", "q_ready", "horner")]
        magnitude, relu, small, ratio = range(4)
        pre = Ring(sem, "l3p", (0, 1, 2, 3), [(f"in{c}", "act") for c in range(DC)])
        proj = Ring(sem, "l3q", (4, 5, 6, 7), [("xd", "act"), ("sp0", None), ("sp1", None), ("sp2", None)]
                    + [(f"dt{c}", "act") for c in range(DC)])
        ln = LayerNorm(g, sem)
        loads = [(w_in_proj, "l3_in"), (ctx_t, "ctx_t"), (w_x, "l3_x"), (conv_w, "l3_conv_w"), (a_neg, "l3_a_log")]
        cols = [(conv_b, "l3_conv_b"), (dt_b, "l3_dt_b"), (skip, "l3_d")]
        n_loads = (len(loads) + len(cols) + 1) * 16
        blk = ph.block()

        @blk.sync
        def _(sp):
            for w, n in loads:
                sp.dma_start(w[:], a[n].rearrange("(c p) n -> p c n", p=P)).then_inc(weights_in, 16)
            for w, n in cols:
                sp.dma_start(w[:], a[n]).then_inc(weights_in, 16)
            sp.dma_start(w_dt[:], a["l3_dt"]).then_inc(weights_in, 16)
            sp.sem_inc(xd_out, 1)
            for b in range(NB):
                sp.wait_ge(xd_ready, b + 1)
                sp.dma_start(xd_dram[b].rearrange("k n l -> (k n) l"), xd[RANK:XD, :]).then_inc(xd_out, 16)
            sp.wait_ge(xd_out, NB * 16 + 1)

        @blk.tensor
        def _(pe):
            pe.wait_ge(weights_in, n_loads)
            with pe.Fori(0, NB) as i:
                for c in range(DC):
                    pre.wait_for(pe, i, free=f"in{c}")
                    pre.fill(product(pe, g["psum"][:, pre.bank(f"in{c}"), :],
                                     [(w_in_proj[:, k, c * P:(c + 1) * P], ctx_t[:, k, bass.ts(i, S)])
                                      for k in range(CC)]))
            pe.wait_ge(u_ready, NB * DC)
            with pe.Fori(0, NB) as i:
                proj.wait_for(pe, i, free="xd")
                proj.fill(product(pe, g["psum"][0:XD, proj.bank("xd"), :],
                                  [(w_x[:, c, :], u[:, c, bass.ts(i, S)]) for c in range(DC)]))
                for c in range(DC):
                    proj.wait_for(pe, i, free=f"dt{c}", drained=["xd"])
                    proj.fill(product(pe, g["psum"][:, proj.bank(f"dt{c}"), :],
                                      [(w_dt[:, c * P:(c + 1) * P], xd[0:RANK, :])]))

        @blk.scalar
        def _(act):
            pre.credit(act, "act")
            proj.credit(act, "act")
            act.wait_ge(pad_ready, 2)
            with act.Fori(0, NB) as i:
                for c in range(DC):
                    if c >= 2:
                        act.wait_ge(conv_done, i * DC + c - 1)
                    pre.wait_filled(act, i, f"in{c}")
                    copy(act, "act", pre, f"in{c}", padded[:, c % 2, TAPS - 1:], g["psum"][:, pre.bank(f"in{c}"), :])
                    if c >= 1:
                        act.wait_ge(conv_done, i * DC + c)
                        act.activation(u[:, c - 1, bass.ts(i, S)], conv[:, (c - 1) % 2, :], ACT.Silu,
                                       bias=conv_b[:, c - 1:c]).then_inc(u_ready, 1)
                act.wait_ge(conv_done, i * DC + DC)
                act.activation(u[:, DC - 1, bass.ts(i, S)], conv[:, (DC - 1) % 2, :], ACT.Silu,
                               bias=conv_b[:, DC - 1:DC]).then_inc(u_ready, 1)
                ln.wait_xn(act, i)
                act.activation(zs[:, :, bass.ts(i, S)], g["xn"][:], ACT.Silu).then_inc(z_ready, 1)
            act.activation(a_neg[:], a_neg[:], ACT.Exp).then_inc(a_exp, 1)
            with act.Fori(0, NB) as i:
                proj.wait_filled(act, i, "xd")
                act.wait_ge(xd_out, i * 16 + 1)
                copy(act, "act", proj, "xd", xd[:], g["psum"][0:XD, proj.bank("xd"), :])
                proj.wait_for(act, i, drained=["xd"])
                act.sem_inc(xd_ready, 1)
                for c in range(DC):
                    act.wait_ge(dt_ready, i * DC + c + 1)
                    bank = g["psum"][:, proj.bank(f"dt{c}"), :]
                    proj.wait_filled(act, i, f"dt{c}")
                    act.activation(soft[:, c, magnitude, :], bank, ACT.Abs, bias=dt_b[:, c:c + 1]).then_inc(soft_act, 1)
                    proj.drain(act.activation(soft[:, c, relu, :], bank, ACT.Relu, bias=dt_b[:, c:c + 1]), f"dt{c}")
                for n, (to, of, func, scale, bias) in enumerate(((small, magnitude, ACT.Exp, -1.0, 0.0),
                                                                 (magnitude, small, ACT.Ln, 1.0, two[:, 0:1]),
                                                                 (ratio, magnitude, ACT.Exp, -1.0, 0.0))):
                    for c in range(DC):
                        act.wait_ge(soft_act, (i * 4 + n) * DC + c + 1)
                        act.activation(soft[:, c, to, :], soft[:, c, of, :], func, scale=scale, bias=bias
                                       ).then_inc(soft_act, 1)
                for c in range(DC):
                    act.wait_ge(s_ready, i * DC + c + 1)
                    act.activation(soft[:, c, magnitude, :], soft[:, c, ratio, :], ACT.Square).then_inc(q_ready, 1)

        @blk.vector
        def _(dve):
            dve.memset(padded[:], 0.0).then_inc(pad_ready, 1)
            ln.credit(dve)
            dve.memset(two[:], 2.0).then_inc(pad_ready, 1)
            dve.wait_ge(weights_in, n_loads)
            st = Steps(conv_steps, DC * (TAPS - 1))
            with dve.Fori(0, NB) as i:
                st.begin(i)
                for c in range(DC):
                    pre.wait_for(dve, i, drained=[f"in{c}"])
                    if c >= 2:
                        dve.wait_ge(u_ready, i * DC + c - 1)
                    p, o = padded[:, c % 2], conv[:, c % 2, :]
                    st.inc(dve.tensor_scalar(o, p[:, 0:S], conv_w[:, c, 0:1], None, ALU.mult))
                    for k in range(1, TAPS):
                        st.wait(dve)
                        ins = dve.scalar_tensor_tensor(o, p[:, k:k + S], conv_w[:, c, k:k + 1], o, ALU.mult, ALU.add)
                        if k < TAPS - 1:
                            st.inc(ins)
                        else:
                            ins.then_inc(conv_done, 1)
                st.end()
                ln.vector(dve, i, (i + 1) & 3, lambda: dve.wait_ge(z_ready, i + 1))
            dve.wait_ge(a_exp, 1)
            dve.tensor_scalar(a_neg[:], a_neg[:], -1.0, None, ALU.mult).then_inc(a_done, 1)
            dve.sem_inc(dt_ready, DC)
            horner_st = Steps(horner, DC * (len(ATANH) - 1))
            with dve.Fori(0, NB) as i:
                horner_st.begin(i)
                for c in range(DC):
                    q, poly, r = soft[:, c, magnitude, :], soft[:, c, small, :], soft[:, c, ratio, :]
                    dve.wait_ge(q_ready, i * DC + c + 1)
                    for k in range(1, len(ATANH)):
                        if k > 1:
                            horner_st.wait(dve)
                        horner_st.inc(dve.scalar_tensor_tensor(
                            poly, poly if k > 1 else q, ATANH[k] / ATANH[0], q if k < len(ATANH) - 1 else r,
                            ALU.add, ALU.mult))
                    horner_st.wait(dve)
                    dve.scalar_tensor_tensor(dt[:, c, bass.ts(i, S)], poly, ATANH[0], soft[:, c, relu, :],
                                             ALU.mult, ALU.add).then_inc(dt_ready, 1)
                horner_st.end()

        @blk.gpsimd
        def _(pool):
            with pool.Fori(0, NB) as i:
                ln.pool(pool, i)
            with pool.Fori(0, NB) as i:
                for c in range(DC):
                    pool.wait_ge(soft_act, (i * 4 + 3) * DC + c + 1)
                    r = soft[:, c, ratio, :]
                    pool.tensor_tensor(r, r, soft[:, c, small, :], ALU.mult).then_inc(s_ready, 1)


def l3_scan(nc, g, u, dt, zs, a_neg, skip, xd_dram):
    with Phase(nc, "l3s") as ph:
        sem, sb = ph.sem, ph.sb
        decay, inflow, product_c = [sb(n, [P, 2, DC, S]) for n in ("decay", "inflow", "product_c")]
        dtu, zero = sb("dtu", [P, DC, S]), sb("zero", [P, DC])
        state = g["xn"]
        rows_b, rows_c = sb("rows_b", [P, 2, S]), sb("rows_c", [P, 2, S])
        last = Ring(sem, "l3y", (4, 5, 6, 7), [(f"o{t}", "dve") for t in range(ST)])
        (dtu_ready, decay_ready, inflow_ready, scan_done, out_done, y_filled, y_read, gated, zero_ready) = [
            sem(n) for n in ("dtu_ready", "decay_ready", "inflow_ready", "scan_done", "out_done", "y_filled", "y_read",
                             "gated", "zero_ready")]
        b_in, c_in = [[sem(f"{n}_in{k}") for k in range(2)] for n in "bc"]
        next_ln = LayerNorm(g, sem)
        blk = ph.block()

        def wait_row(eng, arrived, b, n):
            eng.wait_ge(arrived[n % 2], (b * (NS // 2) + n // 2 + 1) * 16)

        @blk.sync
        def _(sp):
            def load(m, which, rows, arrived, used):
                if m >= 2:
                    sp.wait_ge(used, m - 1)
                sp.dma_start(rows[:, m % 2], xd_dram[m // NS, which, m % NS:m % NS + 1, :].partition_broadcast(P)
                             ).then_inc(arrived[m % 2], 16)

            for m in range(NB * NS + 1):
                if m < NB * NS:
                    load(m, 0, rows_b, b_in, inflow_ready)
                if m >= 1:
                    load(m - 1, 1, rows_c, c_in, out_done)

        @blk.gpsimd
        def _(pool):
            with pool.Fori(0, NB) as b:
                for n in range(NS):
                    if n == 0:
                        pool.wait_ge(dtu_ready, b + 1)
                    wait_row(pool, b_in, b, n)
                    pool.wait_ge(scan_done, b * NS + n + 1)
                    row = rows_b[:, n % 2, :].unsqueeze(1).to_broadcast([P, DC, S])
                    pool.tensor_tensor(inflow[:, n % 2], dtu[:], row,
                                       ALU.mult).then_inc(inflow_ready, 1)
            next_ln.pool(pool, 0)

        @blk.scalar
        def _(act):
            act.wait_ge(zero_ready, 1)
            with act.Fori(0, NB) as b:
                for n in range(NS):
                    act.wait_ge(scan_done, b * NS + n + 1)
                    act.activation(decay[:, n % 2, :, 0], zero[:], ACT.Copy).then_inc(decay_ready, 1)
                    for c in range(DC):
                        act.activation(decay[:, n % 2, c, 1:S], dt[:, c, bass.ds(b * S + 1, S - 1)], ACT.Exp,
                                       scale=a_neg[:, c, n:n + 1]).then_inc(decay_ready, 1)

        @blk.tensor
        def _(pe):
            pe.sem_inc(y_filled, 2)
            with pe.Fori(0, NB) as b:
                for n in range(NS):
                    pe.wait_ge(out_done, b * NS + n + 1)
                    if n == 0:
                        pe.wait_ge(y_read, b * DC + 1)
                    for c in range(DC):
                        ins = pe.matmul(g["psum"][:, c, :], g["ident"][:], product_c[:, n % 2, c, :],
                                        start=(n == 0), stop=(n == NS - 1))
                    ins.then_inc(y_filled, 1)
                pe.wait_ge(gated, (b + 1) * DC)
                for t in range(ST):
                    last.wait_for(pe, b, free=f"o{t}")
                    last.fill(transpose_group(pe, g["psum"][:, last.bank(f"o{t}"), :],
                                              [state[:, c, t * P:(t + 1) * P] for c in range(DC)], g["ident"][:]))

        @blk.vector
        def _(dve):
            dve.memset(zero[:], 0.0).then_inc(zero_ready, 1)
            last.credit(dve, "dve")
            dve.sem_inc(scan_done, 2)
            dve.sem_inc(y_read, 1)

            def dt_times_u(b):
                dve.tensor_tensor(dtu[:], dt[:, :, bass.ts(b, S)],
                                  u[:, :, bass.ts(b, S)], ALU.mult).then_inc(dtu_ready, 1)

            dt_times_u(0)
            with dve.Fori(0, NB) as b:
                for n in range(NS):
                    dve.wait_ge(decay_ready, (b * NS + n + 1) * (DC + 1))
                    dve.wait_ge(inflow_ready, b * NS + n + 1)
                    if n:
                        dve.wait_ge(out_done, b * NS + n)
                    flat = [m.rearrange("p c n -> p (c n)") for m in (state[:], decay[:, n % 2], inflow[:, n % 2])]
                    dve.tensor_tensor_scan(flat[0], flat[1], flat[2], 0.0, ALU.mult, ALU.add).then_inc(scan_done, 1)
                    if n == NS - 1:
                        dt_times_u((b + 1) & 3)
                    dve.wait_ge(scan_done, b * NS + n + 3)
                    row = rows_c[:, n % 2, :].unsqueeze(1).to_broadcast([P, DC, S])
                    wait_row(dve, c_in, b, n)
                    dve.wait_ge(y_filled, b * NS + n + 1)
                    dve.tensor_tensor(product_c[:, n % 2], state[:], row, ALU.mult).then_inc(out_done, 1)
                dve.wait_ge(out_done, (b + 1) * NS)
                dve.wait_ge(y_filled, (b + 1) * NS + 2)
                for c in range(DC):
                    dve.scalar_tensor_tensor(state[:, c, :], u[:, c, bass.ts(b, S)], skip[:, c:c + 1],
                                             g["psum"][:, c, :], ALU.mult, ALU.add).then_inc(y_read, 1)
                for c in range(DC):
                    dve.wait_ge(y_read, b * DC + c + 2)
                    dve.tensor_tensor(state[:, c, :], state[:, c, :], zs[:, c, bass.ts(b, S)], ALU.mult
                                      ).then_inc(gated, 1)
                for t in range(ST):
                    residual(dve, last, b, f"o{t}", g, b * ST + t, g["gate"][:, 3:4])
            last.wait_for(dve, NB - 1, drained=[f"o{ST - 1}"])
            next_ln.vector(dve, 0, 0, lambda: None)


FP8_MAX, FP8_TINY, FP8_STEP = 448.0, 2.0 ** -6, 1.5 * 2 ** 20
EXPONENT = 0x7F800000


def fp8_round(dve, st, amax, inv, v, grid, src, out):
    blocks = src.shape[1]

    def wide(m):
        return m.unsqueeze(2).to_broadcast([P, blocks, P])

    st.inc(dve.tensor_reduce(amax[:, 0, :], src, AX.X, ALU.max, apply_absolute_value=True))
    st.wait(dve)
    st.inc(dve.tensor_scalar(amax[:, 1, :], amax[:, 0, :], 1.0 / FP8_MAX, None, ALU.mult))
    st.wait(dve)
    st.inc(dve.reciprocal(inv, amax[:, 1, :]))
    st.wait(dve)
    st.inc(dve.tensor_tensor(v, src, wide(inv), ALU.mult))
    st.wait(dve)
    st.inc(dve.tensor_scalar(grid.bitcast(I32), v.bitcast(I32), EXPONENT, None, ALU.bitwise_and))
    st.wait(dve)
    st.inc(dve.tensor_scalar(grid, grid, FP8_TINY, FP8_STEP, ALU.max, ALU.mult))
    st.wait(dve)
    st.inc(dve.tensor_tensor(v, v, grid, ALU.add))
    st.wait(dve)
    st.inc(dve.tensor_tensor(v, v, grid, ALU.subtract))
    st.wait(dve)
    st.inc(dve.tensor_tensor(out, v, wide(amax[:, 1, :]), ALU.mult))


FP8_STEPS = 9


def l3_ffn(nc, g, a):
    with Phase(nc, "l3f") as ph:
        sem, sb = ph.sem, ph.sb
        weight = sb("weight", [P, DC, D])
        w_t = sb("w_t", [P, DC, D])
        v, grid = sb("v", [P, 4 * DC, P]), sb("grid", [P, 4 * DC, P])
        x_deq = sb("x_deq", [P, 4 * DC, P])
        amax, inv = sb("amax", [P, 2, 4 * DC]), sb("inv", [P, 4 * DC])
        xt = sb("xt", [P, DC, S])
        (weight_in, w_steps, w_ready, wt_filled, wt_ready, x_steps, x_ready, stored) = [
            sem(n) for n in ("weight_in", "w_steps", "w_ready", "wt_filled", "wt_ready", "x_steps", "x_ready", "stored")]
        ring = Ring(sem, "l3f", range(8), [(f"xt{c}", "act") for c in range(DC)] + [(f"out{t}", "dve") for t in range(ST)])
        ln = LayerNorm(g, sem)
        blk = ph.block()

        @blk.sync
        def _(sp):
            sp.dma_start(weight[:], a["l3_ffn"].rearrange("(c p) n -> p c n", p=P)).then_inc(weight_in, 16)
            for b in range(NB):
                ring.wait_for(sp, b, drained=[f"out{ST - 1}"])
                sp.dma_start(a["out"][b * S:(b + 1) * S, :].rearrange("(t p) d -> p t d", p=P),
                             g["x"][:, b * ST:(b + 1) * ST, :]).then_inc(stored, 16)
            sp.wait_ge(stored, NB * 16)

        @blk.tensor
        def _(pe):
            pe.wait_ge(w_ready, 1)
            for c in range(DC):
                transpose_group(pe, g["psum"][:, c, :], [weight[:, o, c * P:(c + 1) * P] for o in range(DC)],
                                g["ident"][:]).then_inc(wt_filled, 1)
            pe.wait_ge(wt_ready, DC)
            with pe.Fori(0, NB) as i:
                pe.wait_ge(x_ready, i + 1)
                for c in range(DC):
                    ring.wait_for(pe, i, free=f"xt{c}")
                    ring.fill(transpose_group(pe, g["psum"][:, ring.bank(f"xt{c}"), :],
                                              [x_deq[:, s * DC + c, :] for s in range(ST)], g["ident"][:]))
                for t in range(ST):
                    ring.wait_for(pe, i, free=f"out{t}", drained=[f"xt{DC - 1}"])
                    ring.fill(product(pe, g["psum"][:, ring.bank(f"out{t}"), :],
                                      [(xt[:, c, t * P:(t + 1) * P], w_t[:, c, :]) for c in range(DC)]))

        @blk.scalar
        def _(act):
            for c in range(DC):
                act.wait_ge(wt_filled, c + 1)
                act.activation(w_t[:, c, :], g["psum"][:, c, :], ACT.Copy).then_inc(wt_ready, 1)
            ring.credit(act, "act")
            with act.Fori(0, NB) as i:
                for c in range(DC):
                    ring.wait_filled(act, i, f"xt{c}")
                    copy(act, "act", ring, f"xt{c}", xt[:, c, :], g["psum"][:, ring.bank(f"xt{c}"), :])

        @blk.vector
        def _(dve):
            ring.credit(dve, "dve")
            ln.credit(dve)
            st = Steps(w_steps, FP8_STEPS)
            st.begin(0)
            dve.wait_ge(weight_in, 16)
            w = weight[:].rearrange("p c (k n) -> p (c k) n", n=P)
            fp8_round(dve, st, amax, inv[:], v[:], grid[:], w, w)
            st.wait(dve)
            dve.sem_inc(w_ready, 1)
            st = Steps(x_steps, FP8_STEPS)

            def round_x(i):
                st.begin(i)
                fp8_round(dve, st, amax, inv[:], v[:], grid[:], g["xn"][:].rearrange("p s (k n) -> p (s k) n", n=P),
                          x_deq[:])
                st.end()
                st.wait(dve)
                dve.sem_inc(x_ready, 1)

            round_x(0)
            with dve.Fori(0, NB) as i:
                ln.vector(dve, i, (i + 1) & 3, lambda: None)
                ring.wait_filled(dve, i, f"xt{DC - 1}")
                ln.wait_xn(dve, i + 1)
                round_x(i + 1)
                for t in range(ST):
                    residual(dve, ring, i, f"out{t}", g, i * ST + t, g["gate"][:, 7:8])

        @blk.gpsimd
        def _(pool):
            with pool.Fori(0, NB) as i:
                ln.pool(pool, i)


PHASES = [l0_xattn, l0_ffn, l1_xattn, l1_ffn, l2_xattn, l2_ffn, l3_xattn, l3_ffn]


def program(nc, a):
    with ExitStack() as stack:
        def sb(name, shape, dt=F32):
            return stack.enter_context(nc.sbuf_tensor(name, shape, dt))

        g = {
            "x": sb("x_res", [P, NB * ST, D]),
            "xn": sb("xn", [P, ST, D]),
            "ident": sb("ident", [P, P]),
            "ident_bf": sb("ident_bf", [P, P], BF16),
            "ones": sb("ones", [P, P]),
            "gate": sb("gate", [P, 8]),
            "rope": sb("rope", [P, 2, NB * ST, 2, 4]),
            "minus_half": sb("minus_half", [P, 16]), "inv_p": sb("inv_p", [P, 16]), "eps": sb("eps", [P, 16]),
            "ln_stats": sb("ln_stats", [P, ST, 6]),
            "ln_work": sb("ln_work", [P, 8, ST]),
            "psum": stack.enter_context(nc.psum_tensor("psum", [P, 8, 512], F32)),
        }
        setup(nc, g, a)
        for phase in PHASES:
            phase(nc, g, a)


def layout(i):
    def t(n):
        return np.ascontiguousarray(i[n].T)

    arrays = {
        "x": i["x"].reshape(-1, D), "pos": i["fside_BxSx2_0"].reshape(-1, 2),
        "ctx_t": np.ascontiguousarray(i["ctx_1024"].reshape(-1, C).T),
        "g_xattn": i["g_xattn"], "g_ffn": i["g_ffn"],
        "l0_wq": t("L0_xattn_Wq"), "l0_wk": t("L0_xattn_Wk"), "l0_bq": i["L0_xattn_bq"], "l0_bk": i["L0_xattn_bk"],
        "l0_up": t("L0_ffn_W_up"), "l0_down": t("L0_ffn_W_down"), "l0_expert": i["L0_ffn_W_expert"],
        "l0_router": t("L0_ffn_W_gate"),
    }
    had = np.ones((1, 1), np.float32)
    while len(had) < P:
        had = np.block([[had, had], [had, -had]])
    arrays |= {"l1_gate": t("L1_ffn_w_gate"), "l1_up": t("L1_ffn_w_up"), "l1_down": t("L1_ffn_w_down"),
               "hadamard": had}
    arrays |= {"l2_wq": i["L2_xattn_Wq"], "l2_wk": i["L2_xattn_Wk"], "l2_wv": i["L2_xattn_Wv"], "l2_wo": i["L2_xattn_Wo"],
               "l2_gq": i["L2_xattn_gq"], "l2_gk": i["L2_xattn_gk"]}
    def experts(routed, shared):
        return np.ascontiguousarray(np.concatenate([routed.transpose(0, 2, 1),
                                                    shared.reshape(SHARED, I2, D).transpose(0, 2, 1)]))

    arrays |= {
        "l2_router": np.concatenate([i["L2_ffn_w_router"], i["L2_ffn_gate_w"]]).T,
        "l2_ge": experts(i["L2_ffn_wg"], i["L2_ffn_sw_gate"]), "l2_ue": experts(i["L2_ffn_wu"], i["L2_ffn_sw_up"]),
        "l2_de": np.concatenate([i["L2_ffn_wd"].transpose(0, 2, 1), i["L2_ffn_sw_down"].T.reshape(SHARED, I2, D)]),
    }
    arrays |= {
        "l3_in": t("L3_xattn_in_proj_w"), "l3_x": t("L3_xattn_x_proj_w"), "l3_dt": t("L3_xattn_dt_proj_w"),
        "l3_conv_w": i["L3_xattn_conv_w"][:, 0, :], "l3_conv_b": i["L3_xattn_conv_b"].reshape(DC, P).T,
        "l3_dt_b": i["L3_xattn_dt_proj_b"].reshape(DC, P).T, "l3_d": i["L3_xattn_D"].reshape(DC, P).T,
        "l3_a_log": i["L3_xattn_A_log"],
        "l3_ffn": i["L3_ffn_weight"],
    }
    pairs = np.arange(D).reshape(H1, HD // 2, 2).transpose(2, 0, 1).reshape(-1)
    wkv = i["L1_xattn_Wkv"]
    arrays |= {
        "l1_wq": i["L1_xattn_Wq"][:, pairs], "l1_wkv": np.concatenate([wkv[:, :D][:, pairs], wkv[:, D:]], 1),
        "l1_wout": i["L1_xattn_Wout"], "l1_bout": i["L1_xattn_bout"],
    }
    return arrays


def kernel(**inputs):
    import concourse.bacc as bacc
    from concourse.bass_utils import run_bass_kernel_spmd as run

    arrays = layout({k: np.asarray(v) for k, v in inputs.items()})
    nc = bacc.Bacc("TRN2", target_bir_lowering=False, num_devices=1)
    a = {}
    for name, v in arrays.items():
        arrays[name] = np.ascontiguousarray(v)
        a[name] = nc.dram_tensor(name, arrays[name].shape, mybir.dt.from_np(v.dtype), kind="ExternalInput").ap()
    a["out"] = nc.dram_tensor("out", (NB * S, D), F32, kind="ExternalOutput").ap()
    program(nc, a)
    r = run(nc, [arrays], core_ids=[0])
    return r.results[0]["out"].reshape(NB, S, D)
```
